# Optimizing a Trainium2 kernel written in Bass

```python
import numpy as np
import jax
import jax.numpy as jnp

def _softmax(x, axis=-1):
    return jax.nn.softmax(x, axis=axis)

def _gelu(x):
    return jax.nn.gelu(x, approximate=True)

def _silu(x):
    return jax.nn.silu(x)

def _sigmoid(x):
    return jax.nn.sigmoid(x)

def _layernorm(x, axis=-1, eps=1e-05):
    m = jnp.mean(x, axis=axis, keepdims=True)
    v = jnp.var(x, axis=axis, keepdims=True)
    return (x - m) / jnp.sqrt(v + eps)

def _scatter_add(tgt, idx, src, axis=0):
    return tgt.at[idx].add(src)

def _segment_sum(src, seg, n):
    return jax.ops.segment_sum(src, seg, n)
kernel_name = 'mk_decoder_preln_d1_seqx_r4_0e5453'

def setup_inputs(seed: int=0):
    np.random.seed(seed)
    _w = jnp.asarray

    def _rec_inputs():
        import jax
        import jax.numpy as jnp
        _rk = jax.random.key(seed)
        x = 7.22e-05 + 1 * jax.random.normal(jax.random.fold_in(_rk, 1), (8, 512, 256), jnp.float32)
        _lenS = 512 - jax.random.randint(jax.random.fold_in(_rk, 7), (8,), 0, max(1, 512 // 4) + 1, jnp.int32)
        _lenS2 = 512 - jax.random.randint(jax.random.fold_in(_rk, 8), (8,), 0, max(1, 512 // 4) + 1, jnp.int32)
        _ctx_1024P = jax.random.normal(jax.random.fold_in(_rk, 11), (8, 16, 256), jnp.float32)
        _ctx_1024c = jax.random.dirichlet(jax.random.fold_in(_rk, 511), 0.3 * jnp.ones((16,), jnp.float32), (8, 512))
        _ctx_1024t = jnp.einsum('bsk,bkd->bsd', _ctx_1024c, _ctx_1024P)
        _ctx_1024t = _ctx_1024t * jax.lax.rsqrt(jnp.mean(jnp.square(_ctx_1024t)) + 1e-12) * 0.953939
        ctx_1024 = 4.13588e-05 + 0.999923 * (_ctx_1024t + 0.3 * jax.random.normal(jax.random.fold_in(_rk, 611), (8, 512, 256), jnp.float32))
        return (x, ctx_1024)
    x, ctx_1024 = _rec_inputs()

    def _L0_attn_setup():
        import jax, jax.numpy as jnp
        import numpy as np
        EMBED_DIM = 256
        NUM_HEADS = 16
        HEAD_DIM = EMBED_DIM // NUM_HEADS
        SCALING = HEAD_DIM ** (-0.5)
        key = jax.random.key(seed)
        k1, k2, k3, k4, k5 = jax.random.split(key, 5)
        B, S, E, H = (2, 512, EMBED_DIM, NUM_HEADS)
        x = jax.random.normal(k1, (B, S, E), dtype=jnp.float32)
        W_A = jax.random.normal(k2, (H, E), dtype=jnp.float32) * E ** (-0.5)
        W_V = jax.random.normal(k3, (E, E), dtype=jnp.float32) * E ** (-0.5)
        W_O = jax.random.normal(k4, (E, E), dtype=jnp.float32) * E ** (-0.5)
        b_O = jax.random.normal(k5, (E,), dtype=jnp.float32) * 0.01
        return {'x': x, 'W_A': W_A, 'W_V': W_V, 'W_O': W_O, 'b_O': b_O}
    _L0_attn_all = _L0_attn_setup()
    _L0_attn_in = {k: v for k, v in _L0_attn_all.items() if k in ('W_A', 'W_V', 'W_O', 'b_O')}
    del _L0_attn_all

    def _L0_xattn_setup():
        import jax, jax.numpy as jnp
        import numpy as np
        B, S, D_IN, D_OUT = (4, 512, 256, 256)
        USE_MASK = True
        key = jax.random.key(seed)
        ks = jax.random.split(key, 6)
        return {'inputs_for_keys': jax.random.normal(ks[0], (B, S, D_IN), jnp.float32), 'inputs_for_values': jax.random.normal(ks[1], (B, S, D_IN), jnp.float32), 'inputs_for_queries': jax.random.normal(ks[2], (B, S, D_IN), jnp.float32), 'WK': jax.random.normal(ks[3], (D_IN, D_OUT), jnp.float32) * 0.1, 'WV': jax.random.normal(ks[4], (D_IN, D_OUT), jnp.float32) * 0.1, 'WQ': jax.random.normal(ks[5], (D_IN, D_OUT), jnp.float32) * 0.1}
    _L0_xattn_all = _L0_xattn_setup()
    _L0_xattn_in = {k: v for k, v in _L0_xattn_all.items() if k in ('WK', 'WV', 'WQ')}
    del _L0_xattn_all

    def _L0_ffn_setup():
        import jax, jax.numpy as jnp
        import numpy as np
        HIDDEN = 256
        N_ROUTED = 16
        N_SHARED = 2
        TOP_K = 2
        MID_R = HIDDEN // 4
        MID_S = HIDDEN // 2
        key = jax.random.key(seed)
        ks = jax.random.split(key, 8)
        s = 0.02
        return {'x': jax.random.normal(ks[0], (2, 256, HIDDEN), dtype=jnp.float32), 'router_w': jax.random.normal(ks[1], (HIDDEN, N_ROUTED), dtype=jnp.float32) * s, 'wg_r': jax.random.normal(ks[2], (N_ROUTED, HIDDEN, MID_R), dtype=jnp.float32) * s, 'wu_r': jax.random.normal(ks[3], (N_ROUTED, HIDDEN, MID_R), dtype=jnp.float32) * s, 'wd_r': jax.random.normal(ks[4], (N_ROUTED, MID_R, HIDDEN), dtype=jnp.float32) * s, 'wg_s': jax.random.normal(ks[5], (N_SHARED, HIDDEN, MID_S), dtype=jnp.float32) * s, 'wu_s': jax.random.normal(ks[6], (N_SHARED, HIDDEN, MID_S), dtype=jnp.float32) * s, 'wd_s': jax.random.normal(ks[7], (N_SHARED, MID_S, HIDDEN), dtype=jnp.float32) * s}
    _L0_ffn_all = _L0_ffn_setup()
    _L0_ffn_in = {k: v for k, v in _L0_ffn_all.items() if k in ('router_w', 'wg_r', 'wu_r', 'wd_r', 'wg_s', 'wu_s', 'wd_s')}
    del _L0_ffn_all
    return {'x': x, 'ctx_1024': ctx_1024, 'L0_attn_W_A': _L0_attn_in['W_A'], 'L0_attn_W_V': _L0_attn_in['W_V'], 'L0_attn_W_O': _L0_attn_in['W_O'], 'L0_attn_b_O': _L0_attn_in['b_O'], 'L0_xattn_WK': _L0_xattn_in['WK'], 'L0_xattn_WV': _L0_xattn_in['WV'], 'L0_xattn_WQ': _L0_xattn_in['WQ'], 'L0_ffn_router_w': _L0_ffn_in['router_w'], 'L0_ffn_wg_r': _L0_ffn_in['wg_r'], 'L0_ffn_wu_r': _L0_ffn_in['wu_r'], 'L0_ffn_wd_r': _L0_ffn_in['wd_r'], 'L0_ffn_wg_s': _L0_ffn_in['wg_s'], 'L0_ffn_wu_s': _L0_ffn_in['wu_s'], 'L0_ffn_wd_s': _L0_ffn_in['wd_s']}

def reference(x, ctx_1024, L0_attn_W_A, L0_attn_W_V, L0_attn_W_O, L0_attn_b_O, L0_xattn_WK, L0_xattn_WV, L0_xattn_WQ, L0_ffn_router_w, L0_ffn_wg_r, L0_ffn_wu_r, L0_ffn_wd_r, L0_ffn_wg_s, L0_ffn_wu_s, L0_ffn_wd_s):
    import jax
    import jax.numpy as jnp

    def _L0_attn_ref(x, W_A, W_V, W_O, b_O):
        import jax, jax.numpy as jnp
        import numpy as np
        EMBED_DIM = 256
        NUM_HEADS = 16
        HEAD_DIM = EMBED_DIM // NUM_HEADS
        SCALING = HEAD_DIM ** (-0.5)
        B, S, E = x.shape
        H, D = (NUM_HEADS, HEAD_DIM)
        z = jnp.einsum('bse,he->bsh', x, W_A) * SCALING
        z = jax.nn.softmax(z, axis=1)
        zp = jnp.transpose(z, (0, 2, 1))
        i = jnp.arange(S)[:, None]
        j = jnp.arange(S)[None, :]
        idx = (i - j) % S
        tril = (j <= i).astype(x.dtype)
        roll = zp[:, :, idx] * tril
        v = jnp.einsum('bse,fe->bsf', x, W_V).reshape(B, S, H, D)
        out = jnp.einsum('bhij,bjhd->bihd', roll, v).reshape(B, S, E)
        return jnp.einsum('bse,fe->bsf', out, W_O) + b_O

    def _L0_xattn_ref(inputs_for_keys, inputs_for_values, inputs_for_queries, WK, WV, WQ):
        import jax, jax.numpy as jnp
        import numpy as np
        B, S, D_IN, D_OUT = (4, 512, 256, 256)
        USE_MASK = True
        K = jnp.einsum('bsd,de->bse', inputs_for_keys, WK)
        V = jnp.einsum('bsd,de->bse', inputs_for_values, WV)
        Q = jnp.einsum('bsd,de->bse', inputs_for_queries, WQ)
        dk = jnp.asarray(K.shape[2], jnp.float32)
        score = jnp.einsum('bqd,bkd->bqk', Q, K) / jnp.sqrt(dk)
        if USE_MASK:
            q_idx = jnp.arange(S)[:, None]
            k_idx = jnp.arange(S)[None, :]
            mask = jnp.where(k_idx > q_idx, -jnp.inf, 0.0).astype(score.dtype)
            score = score + mask[None, :, :]
        soft_score = jax.nn.softmax(score, axis=-1)
        return jnp.einsum('bqk,bkd->bqd', soft_score, V)

    def _L0_ffn_ref(x, router_w, wg_r, wu_r, wd_r, wg_s, wu_s, wd_s):
        import jax, jax.numpy as jnp
        import numpy as np
        HIDDEN = 256
        N_ROUTED = 16
        N_SHARED = 2
        TOP_K = 2
        MID_R = HIDDEN // 4
        MID_S = HIDDEN // 2
        orig_shape = x.shape
        flat = x.reshape(-1, orig_shape[-1])
        gs = jnp.einsum('td,ndm->tnm', flat, wg_s)
        us = jnp.einsum('td,ndm->tnm', flat, wu_s)
        out = jnp.einsum('tnm,nmd->td', jax.nn.silu(gs) * us, wd_s)
        logits = (flat @ router_w).astype(jnp.float32)
        probs = jax.nn.softmax(logits, axis=-1)
        weights, indices = jax.lax.top_k(probs, TOP_K)
        weights = weights / (weights.sum(axis=-1, keepdims=True) + 1e-09)
        weights = weights.astype(x.dtype)
        comb = jnp.sum(jax.nn.one_hot(indices, N_ROUTED, dtype=x.dtype) * weights[..., None], axis=1)
        g = jnp.einsum('td,edm->tem', flat, wg_r)
        u = jnp.einsum('td,edm->tem', flat, wu_r)
        h = jax.nn.silu(g) * u
        h = h * comb[:, :, None]
        out = out + jnp.einsum('tem,emd->td', h, wd_r)
        return out.reshape(orig_shape)
    x = x + _L0_attn_ref(_layernorm(x, axis=-1), L0_attn_W_A, L0_attn_W_V, L0_attn_W_O, L0_attn_b_O)
    x = x + _L0_xattn_ref(_layernorm(x, axis=-1), ctx_1024, ctx_1024, L0_xattn_WK, L0_xattn_WV, L0_xattn_WQ)
    x = x + _L0_ffn_ref(_layernorm(x, axis=-1), L0_ffn_router_w, L0_ffn_wg_r, L0_ffn_wu_r, L0_ffn_wd_r, L0_ffn_wg_s, L0_ffn_wu_s, L0_ffn_wd_s)
    return x

_drawn_inputs = setup_inputs


def setup_inputs(seed=0):
    import zlib

    import numpy as np

    out = dict(_drawn_inputs(seed))
    spreads = {}
    factors = {'L0_attn_b_O': 8.0,
     'L0_ffn_router_w': 8.0,
     'L0_ffn_wg_r': 8.0,
     'L0_ffn_wu_r': 8.0,
     'L0_ffn_wd_r': 8.0,
     'L0_ffn_wg_s': 4.813,
     'L0_ffn_wu_s': 4.722,
     'L0_ffn_wd_s': 4.782}
    for name, (base, spread) in spreads.items():
        noise = np.random.default_rng([zlib.crc32(name.encode()), seed]).standard_normal(out[name].shape)
        drawn = base * np.exp(spread * noise) if base else spread * noise
        out[name] = jnp.asarray(drawn.astype(out[name].dtype))
    for name, factor in factors.items():
        out[name] = (out[name] * factor).astype(out[name].dtype)
    return out
```

```python
from contextlib import ExitStack

import concourse.bass as bass
from concourse import mybir

P = 128
ALU = mybir.AluOpType
ACT = mybir.ActivationFunctionType
AX = mybir.AxisListType
F32 = mybir.dt.float32
F32R = mybir.dt.float32r
F16 = mybir.dt.float16
BF16 = mybir.dt.bfloat16
U32 = mybir.dt.uint32

B, S, E = 8, 512, 256
H, D = 16, 16
NE, MR = 16, 64
C = S // P
K2 = E // P
NSH = 2
PAIRS = NE * MR // P
MID = NSH + PAIRS
PAD = P
ZROW = PAD + S
ZSCALE = 4096.0
EPS = 1e-5
NEG = -1e30


class Signal:

    def __init__(self, sem, per_batch, before=0):
        self.sem, self.per_batch, self.before = sem, per_batch, before

    def at(self, batch, count):
        return batch * self.per_batch + (count + self.before)


def three_passes(pe, out, stationary, moving, start, stop, **kw):
    pe.matmul(out, stationary[0], moving[0], start=start, stop=False, **kw)
    pe.matmul(out, stationary[0], moving[1], start=False, stop=False, **kw)
    return pe.matmul(out, stationary[1], moving[0], start=False, stop=stop, **kw)


def decoder_layer(nc, x, ctxT, wa, wv, wo, bo, wq, wk, wvx, rw, gu_s, wd_s, gu_r, wd_r, out):
    with ExitStack() as ctx:
        def sb(name, shape, dt=F32):
            return ctx.enter_context(nc.sbuf_tensor(name, shape, dt))

        def bank(name, shape=(P, 512), dt=F32):
            return ctx.enter_context(nc.psum_tensor(name, list(shape), dt))

        def sem(name):
            return ctx.enter_context(nc.semaphore(name))

        def sig(name, per_batch, before=0):
            return Signal(sem(name), per_batch, before)

        w_a = sb("w_a", [P, 2, K2, P], F32R)
        w_v = sb("w_v", [P, 2, K2, E], F32R)
        w_o = sb("w_o", [P, 2, K2, E], F32R)
        w_qk = sb("w_qk", [P, 2, K2, E], F32R)
        w_vx = sb("w_vx", [P, 2, K2, E], F32R)
        w_r = sb("w_r", [P, 2, K2, NE], F32R)
        w_gu = sb("w_gu", [P, 2, K2, 2 * MID * P], F32R)
        w_d = sb("w_d", [P, 2, MID, E], F32R)

        ident = sb("ident", [P, P])
        ident16 = sb("ident16", [P, P], BF16)
        future = sb("future", [P, P], BF16)
        expert_no_i = sb("expert_no_i", [P, NE], mybir.dt.int32)
        expert_no = sb("expert_no", [P, NE])
        spread = sb("spread", [NE, PAIRS, P])
        zeros16 = sb("zeros16", [2 * H, PAD], F16)
        b_o = sb("b_o", [P, E])

        x_in = sb("x_in", [P, C, E])
        x_bo = sb("x_bo", [P, C, E])
        x_res = sb("x_res", [P, C, E])
        stats = sb("stats", [P, C, 6])
        mean_var = sb("mean_var", [P, C, 2])
        rstd = sb("rstd", [P, C])
        var_eps = sb("var_eps", [P, C])
        minus_half = sb("minus_half", [P, C])
        h = sb("h", [P, C, E])
        hT = sb("hT", [P, 2, K2, S], F32R)
        z_nmax = sb("z_nmax", [P, 1])
        z_exp = sb("z_exp", [P, S])
        z_sum = sb("z_sum", [P, 1])
        z_rsum = sb("z_rsum", [P, 1])
        z_norm = sb("z_norm", [P, S])
        z_parts = sb("z_parts", [P, 2, S], F16)
        toep = sb("toep", [P, 2, H, S], F16)
        val = sb("val", [P, 2, H, C, D], F16)
        mix = sb("mix", [P, C, E])
        cT_in = sb("cT_in", [P, K2, S])
        cT = sb("cT", [P, 2, K2, S], F32R)
        vx = sb("vx", [P, 2, C, E], F32R)
        qT = sb("qT", [P, 2, K2, S], F32R)
        s_nmax = sb("s_nmax", [P, C])
        s_sum = sb("s_sum", [P, C])
        s_rsum = sb("s_rsum", [P, C])
        prob = sb("prob", [P, 2, S])
        probT = sb("probT", [P, 2, 2, S], F32R)
        logit = sb("logit", [P, C, NE])
        top = sb("top", [P, C, 8])
        top_i = sb("top_i", [P, C, 8], U32)
        top_f = sb("top_f", [P, C, 2])
        l_shift = sb("l_shift", [P, C, NE])
        l_exp = sb("l_exp", [P, C, NE])
        e2_in = sb("e2_in", [P, C])
        e2 = sb("e2", [P, C])
        l_sum = sb("l_sum", [P, C])
        w_den = sb("w_den", [P, C])
        w_den2 = sb("w_den2", [P, C])
        w_one = sb("w_one", [P, C])
        w_1 = sb("w_1", [P, C])
        w_2 = sb("w_2", [P, C])
        comb1 = sb("comb1", [P, C, NE])
        comb2 = sb("comb2", [P, C, NE])
        comb = sb("comb", [P, C, NE])
        combT = sb("combT", [NE, S])
        th = sb("th", [P, 2, S])
        gt = gtu = midc = th
        mid = probT

        turned = [bank(f"turned{k}") for k in range(2)]
        score = [bank(f"score{k}") for k in range(2)]
        wide = bank("wide", [P, 2, 512])
        rows = [bank(f"rows{k}") for k in range(2)]

        stage = toep[:].rearrange("p a h s -> p (a h s)").bitcast(F32)

        z_dram = nc.dram_tensor("z_scratch", [B, 2 * H, ZROW], F16, kind="Internal").ap()

        w_loaded = sem("w_loaded")
        gu_loaded = sem("gu_loaded")
        w_hi = sem("w_hi")
        w_lo = sem("w_lo")
        const_made = sem("const_made")
        wa_zeroed = sem("wa_zeroed")
        qk_product = sem("qk_product")
        pads_stored = sem("pads_stored")
        bo_loaded = sem("bo_loaded")

        held = {eng.engine: sem(f"held_{n}") for n, eng in (("dve", nc.vector), ("pool", nc.gpsimd))}
        x_loaded = sig("x_loaded", 16)
        c_loaded = sig("c_loaded", 16)
        z_stored = sig("z_stored", 16)
        toep_loaded = sig("toep_loaded", 32)
        y_stored = sig("y_stored", 16, 16)
        x_biased = sig("x_biased", 1, 1)
        c_hi = sig("c_hi", 1)
        c_split = sig("c_split", 1, 1)
        stats_done = sig("stats_done", 3)
        aggr_done = sig("aggr_done", 3)
        eps_added = sig("eps_added", 3)
        rstd_done = sig("rstd_done", 3)
        h_ready = sig("h_ready", 3, 3)
        turned_ready = sig("turned_ready", 8, 1)
        hT_hi = sig("hT_hi", 8)
        hT_ready = sig("hT_ready", 8, 1)
        hT_used = sig("hT_used", 4, 1)
        z_ready = sig("z_ready", 1)
        z_maxed = sig("z_maxed", 1)
        z_exped = sig("z_exped", 1)
        z_recip = sig("z_recip", 1)
        z_scaled = sig("z_scaled", 2)
        z_split = sig("z_split", 1)
        rows_ready = sig("rows_ready", 16)
        rows_hi = sig("rows_hi", 8)
        rows_taken = sig("rows_taken", 16, 2)
        toep_used = sig("toep_used", 1, 1)
        vals_used = sig("vals_used", 1, 1)
        mix_ready = sig("mix_ready", 2)
        mix_taken = sig("mix_taken", 2)
        q_ready = sig("q_ready", 2)
        q_hi = sig("q_hi", 2)
        q_split = sig("q_split", 2)
        q_used = sig("q_used", 1, 1)
        c_used = sig("c_used", 1, 1)
        score_ready = sig("score_ready", 4)
        score_maxed = sig("score_maxed", 4)
        prob_ready = sig("prob_ready", 4, 1)
        prob_recip = sig("prob_recip", 4)
        probT_ready = sig("probT_ready", 4, 1)
        probT_hi = sig("probT_hi", 4)
        probT_split = sig("probT_split", 4, 1)
        probT_used = sig("probT_used", 4, 2)
        logit_ready = sig("logit_ready", 1)
        logit_copied = sig("logit_copied", 1)
        topped = sig("topped", 1)
        top_found = sig("top_found", 1)
        shifted = sig("shifted", 2)
        l_exped = sig("l_exped", 2)
        weigh = sig("weigh", 9)
        combT_ready = sig("combT_ready", 1)
        combT_copied = sig("combT_copied", 1)
        g_ready = sig("g_ready", MID)
        u_ready = sig("u_ready", MID)
        comb_ready = sig("comb_ready", PAIRS)
        tanh_done = sig("tanh_done", MID)
        gt_done = sig("gt_done", MID)
        gtu_done = sig("gtu_done", MID, 1)
        midc_done = sig("midc_done", PAIRS, 1)
        mid_hi = sig("mid_hi", MID)
        mid_split = sig("mid_split", MID)
        mid_used = sig("mid_used", MID, 2)
        y_ready = sig("y_ready", 1)
        y_taken = sig("y_taken", 1, 1)

        small = [
            (wv.rearrange("(k p) n -> p k n", p=P), w_v, K2, E),
            (wa.rearrange("(k p) n -> p k n", p=P), w_a, K2, H),
            (wo.rearrange("(k p) n -> p k n", p=P), w_o, K2, E),
            (wvx.rearrange("(k p) n -> p k n", p=P), w_vx, K2, E),
            (wq.rearrange("(k p) n -> p k n", p=P), w_gu[:, :, :, 0:E], K2, E),
            (wk.rearrange("(k p) n -> p k n", p=P), w_gu[:, :, :, E:2 * E], K2, E),
            (rw.rearrange("(k p) n -> p k n", p=P), w_r, K2, NE),
            (wd_s.rearrange("(j p) n -> p j n", p=P), w_d[:, :, 0:NSH, :], NSH, E),
            (wd_r.rearrange("(j p) n -> p j n", p=P), w_d[:, :, NSH:MID, :], PAIRS, E),
        ]
        at, pieces = 0, []
        for src, dst, k, n in small:
            pieces.append((src, dst, stage[:, at:at + k * n].rearrange("p (k n) -> p k n", k=k), n))
            at += k * n
        assert at <= 8192
        NS, NC = NSH * P * 2, NE * MR * 2
        second = [
            (gu_s.rearrange("(k p) n -> p k n", p=P), w_gu[:, :, :, 0:NS], 0, NS),
            (gu_r.rearrange("(k p) n -> p k n", p=P), w_gu[:, :, :, NS:NS + NC], 1024, NC),
        ]
        big = [(src, dst, stage[:, o:o + K2 * n].rearrange("p (k n) -> p k n", k=K2), n)
               for src, dst, o, n in second]
        SCALED = {1: 0.25}
        FIRST_ROUND = len(pieces)
        SPLITS = FIRST_ROUND + len(big) + 2

        def hold(eng, signal, value):
            eng.wait_ge(signal.sem, value)
            eng.sem_inc(held[eng.engine], 1)

        def backwards(row):
            return row.rearrange("p (c t) -> p c t", t=P)[:, :, ::-1]

        def parts(t, *index):
            return [t[(slice(None), a, *index)] for a in range(2)]

        block = ctx.enter_context(nc.Block())

        @block.sync
        def _(sp):
            sp.dma_start(b_o[:], bo.partition_broadcast(P)).then_inc(bo_loaded, 16)
            for src, _, at, _ in pieces:
                sp.dma_start(at, src).then_inc(w_loaded, 16)
            sp.wait_ge(w_lo, FIRST_ROUND + 2)
            for src, _, at, _ in big:
                sp.dma_start(at, src).then_inc(gu_loaded, 16)
            sp.wait_ge(const_made, 1)
            for b in range(B):
                sp.dma_start(z_dram[b, :, 0:PAD], zeros16[:]).then_inc(pads_stored, 16)
            with sp.Fori(0, B) as b:
                sp.wait_ge(x_biased.sem, x_biased.at(b, 0))
                sp.wait_ge(h_ready.sem, h_ready.at(b, -2))
                sp.dma_start(x_in[:], x[b].rearrange("(c p) e -> p c e", p=P)).then_inc(x_loaded.sem, 16)
                sp.wait_ge(c_split.sem, c_split.at(b, 0))
                sp.dma_start(cT_in[:], ctxT[b].rearrange("(k p) s -> p k s", p=P)).then_inc(c_loaded.sem, 16)

        @block.gpsimd
        def _(pool):
            pool.memset(zeros16[:], 0.0).then_inc(const_made, 1)
            pool.memset(ident[:], 0.0).then_inc(const_made, 1)
            pool.memset(future[:], 0.0).then_inc(const_made, 1)
            pool.memset(spread[:], 0.0).then_inc(const_made, 1)
            pool.iota(expert_no_i[:], pattern=[[1, NE]], base=0, channel_multiplier=0).then_inc(const_made, 1)
            pool.memset(minus_half[:], -0.5).then_inc(const_made, 1)
            pool.wait_ge(const_made, 6)
            pool.affine_select(out=ident[:], in_=ident[:], compare_op=ALU.not_equal, fill=1.0, base=0,
                               pattern=[[-1, P]], channel_multiplier=1).then_inc(const_made, 1)
            pool.affine_select(out=future[:], in_=future[:], compare_op=ALU.is_ge, fill=NEG, base=0,
                               pattern=[[-1, P]], channel_multiplier=1).then_inc(const_made, 1)
            sp4 = spread[:].rearrange("e q (g m) -> e q g m", g=2)
            pool.affine_select(out=sp4, in_=sp4, compare_op=ALU.not_equal, fill=1.0, base=0,
                               pattern=[[-2, PAIRS], [-1, 2], [0, MR]], channel_multiplier=1).then_inc(const_made, 1)
            pool.tensor_copy(expert_no[:], expert_no_i[:]).then_inc(const_made, 1)
            pool.wait_ge(const_made, 10)
            pool.tensor_copy(ident16[:], ident[:]).then_inc(const_made, 1)
            pool.wait_ge(bo_loaded, 16)
            pool.sem_inc(x_biased.sem, 1)
            pool.sem_inc(c_split.sem, 1)
            def reciprocal_deviation(b, n):
                hold(pool, aggr_done, aggr_done.at(b, n + 1))
                pool.tensor_scalar(var_eps[:], mean_var[:, :, 1], EPS, None, ALU.add).then_inc(eps_added.sem, 1)
                pool.wait_ge(eps_added.sem, eps_added.at(b, n + 1))
                pool.tensor_tensor(rstd[:], var_eps[:], minus_half[:], ALU.pow).then_inc(rstd_done.sem, 1)

            with pool.Fori(0, B) as b:
                pool.wait_ge(x_loaded.sem, x_loaded.at(b, 16))
                pool.wait_ge(rows_taken.sem, rows_taken.at(b, 0))
                for c in range(C):
                    last = pool.tensor_tensor(x_bo[:, c, :], x_in[:, c, :], b_o[:], ALU.add)
                last.then_inc(x_biased.sem, 1)
                reciprocal_deviation(b, 0)
                pool.wait_ge(c_loaded.sem, c_loaded.at(b, 16))
                hold(pool, c_used, c_used.at(b, 0))
                pool.tensor_copy(cT[:, 0], cT_in[:]).then_inc(c_hi.sem, 1)
                pool.wait_ge(c_hi.sem, c_hi.at(b, 1))
                pool.tensor_tensor(cT[:, 1], cT_in[:], cT[:, 0], ALU.subtract).then_inc(c_split.sem, 1)
                reciprocal_deviation(b, 1)
                reciprocal_deviation(b, 2)

        @block.scalar
        def _(act):
            act.wait_ge(wa_zeroed, 1)
            for n, (_, dst, at, w) in enumerate(pieces):
                act.wait_ge(w_loaded, 16 * len(pieces))
                act.activation(dst[:, 0, :, 0:w], at, ACT.Copy, scale=SCALED.get(n, 1.0)).then_inc(w_hi, 1)
            for k in range(K2):
                act.wait_ge(qk_product, k + 1)
                act.activation(w_qk[:, 0, k], rows[k][:, 0:E], ACT.Copy, scale=E ** -0.5).then_inc(w_hi, 1)
            act.wait_ge(gu_loaded, 16 * len(big))
            for _, dst, at, w in big:
                act.activation(dst[:, 0], at, ACT.Copy).then_inc(w_hi, 1)

            def turn(b, n):
                act.wait_ge(hT_used.sem, hT_used.at(b, n))
                for k in range(K2):
                    act.wait_ge(turned_ready.sem, turned_ready.at(b, 2 * n + k + 1))
                    act.activation(hT[:, 0, k], backwards(turned[k][:]) if n == 0 else turned[k][:], ACT.Copy).then_inc(hT_hi.sem, 1)

            act.sem_inc(prob_ready.sem, 1)
            act.sem_inc(y_stored.sem, 16)
            with act.Fori(0, B) as b:
                turn(b, 0)
                act.wait_ge(z_maxed.sem, z_maxed.at(b, 1))
                act.activation(z_exp[0:H, :], backwards(score[0][0:H, :]), ACT.Exp, bias=z_nmax[0:H, :],
                               accum_out=z_sum[0:H, :]).then_inc(z_exped.sem, 1)
                act.wait_ge(vals_used.sem, vals_used.at(b, 0))
                for c in range(C):
                    act.wait_ge(rows_ready.sem, rows_ready.at(b, c + 1))
                    act.activation(val[:, 0, :, c, :], rows[c % 2][:, 0:E].rearrange("p (h d) -> p h d", h=H),
                                   ACT.Copy).then_inc(rows_hi.sem, 1)
                act.wait_ge(z_split.sem, z_split.at(b, 1))
                act.dma_start(z_dram[b, :, PAD:ZROW].rearrange("(a h) s -> h a s", a=2),
                              z_parts[0:H]).then_inc(z_stored.sem, 16)
                act.wait_ge(z_stored.sem, z_stored.at(b, 16))
                act.wait_ge(pads_stored, 16 * B)
                act.wait_ge(w_lo, SPLITS)
                act.wait_ge(toep_used.sem, toep_used.at(b, 0))
                for a in range(2):
                    src = z_dram[b, a * H:(a + 1) * H, PAD - P + 1:ZROW]
                    skewed = bass.AP(src.tensor, src.offset, [[1, P], [ZROW, H], [1, S]])
                    act.dma_start(toep[:, a], skewed).then_inc(toep_loaded.sem, 16)
                for c in range(C):
                    act.wait_ge(rows_ready.sem, rows_ready.at(b, C + c + 1))
                    if c == 0:
                        act.wait_ge(q_used.sem, q_used.at(b, 0))
                    act.activation(vx[:, 0, c], rows[c % 2][:, 0:E], ACT.Copy).then_inc(rows_hi.sem, 1)
                for k in range(K2):
                    act.wait_ge(q_ready.sem, q_ready.at(b, k + 1))
                    act.wait_ge(q_used.sem, q_used.at(b, 0))
                    act.activation(qT[:, 0, k], wide[:, k], ACT.Copy).then_inc(q_hi.sem, 1)
                for g in range(2):
                    act.wait_ge(mix_ready.sem, mix_ready.at(b, g + 1))
                    if g == 0:
                        act.wait_ge(turned_ready.sem, turned_ready.at(b, 2))
                    act.activation(
                        mix[:, :, P * g:P * g + P].rearrange("p c (h d) -> p h c d", d=D),
                        wide[:, g].rearrange("p (h c d) -> p h c d", c=C, d=D),
                        ACT.Copy, scale=1.0 / ZSCALE).then_inc(mix_taken.sem, 1)
                turn(b, 1)
                turn(b, 2)

                def part_prob(c):
                    act.wait_ge(probT_ready.sem, probT_ready.at(b, c + 1))
                    act.wait_ge(probT_used.sem, probT_used.at(b, c - 1))
                    act.activation(probT[:, 0, c % 2, 0:P * (c + 1)], turned[c % 2][:, 0:P * (c + 1)],
                                   ACT.Copy).then_inc(probT_hi.sem, 1)

                act.wait_ge(mid_used.sem, mid_used.at(b, 0))
                for c in range(C):
                    n = P * (c + 1)
                    act.wait_ge(score_maxed.sem, score_maxed.at(b, c + 1))
                    act.wait_ge(probT_ready.sem, probT_ready.at(b, max(c - 1, 0)))
                    act.activation(prob[:, c % 2, 0:n], score[c % 2][:, 0:n], ACT.Exp, bias=s_nmax[:, c:c + 1],
                                   accum_out=s_sum[:, c:c + 1]).then_inc(prob_ready.sem, 1)
                    if c:
                        part_prob(c - 1)
                part_prob(C - 1)
                turn(b, 3)
                act.wait_ge(shifted.sem, shifted.at(b, 1))
                act.activation(e2[:], e2_in[:], ACT.Exp).then_inc(l_exped.sem, 1)
                act.wait_ge(shifted.sem, shifted.at(b, 2))
                act.activation(l_exp[:], l_shift[:], ACT.Exp).then_inc(l_exped.sem, 1)

                def part_mid(j):
                    act.wait_ge(mid_used.sem, mid_used.at(b, j))
                    if j < NSH:
                        act.wait_ge(gtu_done.sem, gtu_done.at(b, j + 1))
                        act.activation(mid[:, 0, j % 2], gtu[:, j % 2], ACT.Copy, scale=0.5).then_inc(mid_hi.sem, 1)
                    else:
                        act.wait_ge(midc_done.sem, midc_done.at(b, j - NSH + 1))
                        act.activation(mid[:, 0, j % 2], midc[:, j % 2], ACT.Copy).then_inc(mid_hi.sem, 1)

                act.wait_ge(probT_used.sem, probT_used.at(b, C))
                for j in range(MID):
                    act.wait_ge(g_ready.sem, g_ready.at(b, j + 1))
                    if j >= 2:
                        act.wait_ge(mid_split.sem, mid_split.at(b, j - 1))
                    act.activation(th[:, j % 2], score[j % 2][:], ACT.Tanh, scale=0.5).then_inc(tanh_done.sem, 1)
                    if j:
                        part_mid(j - 1)
                part_mid(MID - 1)
                act.wait_ge(y_taken.sem, y_taken.at(b, 1))
                act.dma_start(out[b].rearrange("(c p) e -> p c e", p=P), x_res[:]).then_inc(y_stored.sem, 16)
            act.wait_ge(y_stored.sem, y_stored.at(B, 0))

        @block.vector
        def _(dve):
            dve.memset(w_a[:].bitcast(F32), 0.0).then_inc(wa_zeroed, 1)
            for n, (_, dst, at, w) in enumerate(pieces):
                dve.wait_ge(w_hi, n + 1)
                dve.scalar_tensor_tensor(dst[:, 1, :, 0:w], at, SCALED.get(n, 1.0), dst[:, 0, :, 0:w],
                                         ALU.mult, ALU.subtract).then_inc(w_lo, 1)
            for k in range(K2):
                dve.wait_ge(w_hi, FIRST_ROUND + k + 1)
                dve.scalar_tensor_tensor(w_qk[:, 1, k], rows[k][:, 0:E], E ** -0.5, w_qk[:, 0, k],
                                         ALU.mult, ALU.subtract).then_inc(w_lo, 1)
            for n, (_, dst, at, w) in enumerate(big):
                dve.wait_ge(w_hi, FIRST_ROUND + 2 + n + 1)
                dve.tensor_tensor(dst[:, 1], at, dst[:, 0], ALU.subtract).then_inc(w_lo, 1)
            dve.sem_inc(hT_ready.sem, 1)
            dve.sem_inc(h_ready.sem, 3)
            dve.sem_inc(rows_taken.sem, 2)
            dve.sem_inc(probT_split.sem, 1)
            dve.sem_inc(gtu_done.sem, 1)
            dve.sem_inc(midc_done.sem, 1)
            dve.sem_inc(y_taken.sem, 1)

            def layernorm(b, n, src):
                for c in range(C):
                    last = dve.bn_stats(stats[:, c], src[:, c])
                last.then_inc(stats_done.sem, 1)
                hold(dve, stats_done, stats_done.at(b, n + 1))
                for c in range(C):
                    last = dve.bn_aggr(mean_var[:, c], stats[:, c])
                last.then_inc(aggr_done.sem, 1)
                dve.wait_ge(rstd_done.sem, rstd_done.at(b, n + 1))
                if n == 0:
                    dve.wait_ge(turned_ready.sem, turned_ready.at(b, 0))
                else:
                    dve.wait_ge(turned_ready.sem, turned_ready.at(b, 2 * n))
                for c in range(C):
                    last = dve.tensor_scalar(h[:, c], src[:, c], mean_var[:, c, 0:1], rstd[:, c:c + 1],
                                             ALU.subtract, ALU.mult)
                last.then_inc(h_ready.sem, 1)

            def turn(b, n):
                for k in range(K2):
                    dve.wait_ge(hT_hi.sem, hT_hi.at(b, 2 * n + k + 1))
                    dve.tensor_tensor(hT[:, 1, k], backwards(turned[k][:]) if n == 0 else turned[k][:], hT[:, 0, k],
                                      ALU.subtract).then_inc(hT_ready.sem, 1)

            with dve.Fori(0, B) as b:
                dve.wait_ge(x_loaded.sem, x_loaded.at(b, 16))
                layernorm(b, 0, x_in)
                turn(b, 0)
                dve.wait_ge(z_ready.sem, z_ready.at(b, 1))
                dve.reduce_max(z_nmax[0:H, :], score[0][0:H, :], AX.X, negate=True).then_inc(z_maxed.sem, 1)
                for c in range(2):
                    dve.wait_ge(rows_hi.sem, rows_hi.at(b, c + 1))
                    dve.tensor_tensor(val[:, 1, :, c, :], rows[c % 2][:, 0:E].rearrange("p (h d) -> p h d", h=H),
                                      val[:, 0, :, c, :], ALU.subtract).then_inc(rows_taken.sem, 1)
                dve.wait_ge(z_exped.sem, z_exped.at(b, 1))
                dve.reciprocal(z_rsum[0:H, :], z_sum[0:H, :]).then_inc(z_recip.sem, 1)
                dve.wait_ge(z_recip.sem, z_recip.at(b, 1))
                dve.tensor_scalar(z_norm[0:H, :], z_exp[0:H, :], z_rsum[0:H, :], ZSCALE, ALU.mult,
                                  ALU.mult).then_inc(z_scaled.sem, 1)
                dve.wait_ge(z_scaled.sem, z_scaled.at(b, 1))
                dve.tensor_copy(z_parts[0:H, 0, :], z_norm[0:H, :]).then_inc(z_scaled.sem, 1)
                dve.wait_ge(z_scaled.sem, z_scaled.at(b, 2))
                dve.tensor_tensor(z_parts[0:H, 1, :], z_norm[0:H, :], z_parts[0:H, 0, :],
                                  ALU.subtract).then_inc(z_split.sem, 1)
                for c in range(2, C):
                    dve.wait_ge(rows_hi.sem, rows_hi.at(b, c + 1))
                    dve.tensor_tensor(val[:, 1, :, c, :], rows[c % 2][:, 0:E].rearrange("p (h d) -> p h d", h=H),
                                      val[:, 0, :, c, :], ALU.subtract).then_inc(rows_taken.sem, 1)
                for c in range(C):
                    dve.wait_ge(rows_hi.sem, rows_hi.at(b, C + c + 1))
                    dve.tensor_tensor(vx[:, 1, c], rows[c % 2][:, 0:E], vx[:, 0, c],
                                      ALU.subtract).then_inc(rows_taken.sem, 1)
                for k in range(K2):
                    dve.wait_ge(q_hi.sem, q_hi.at(b, k + 1))
                    dve.tensor_tensor(qT[:, 1, k], wide[:, k], qT[:, 0, k], ALU.subtract).then_inc(q_split.sem, 1)
                turn(b, 1)
                dve.wait_ge(y_stored.sem, y_stored.at(b, 0))
                dve.wait_ge(x_biased.sem, x_biased.at(b, 1))
                for c in range(C):
                    dve.wait_ge(rows_ready.sem, rows_ready.at(b, 2 * C + c + 1))
                    dve.tensor_tensor(x_res[:, c], rows[c % 2][:, 0:E], x_bo[:, c],
                                      ALU.add).then_inc(rows_taken.sem, 1)
                dve.wait_ge(rows_taken.sem, rows_taken.at(b, 3 * C))
                layernorm(b, 1, x_res)
                turn(b, 2)

                def score_max(c):
                    dve.wait_ge(score_ready.sem, score_ready.at(b, c + 1))
                    dve.reduce_max(s_nmax[:, c:c + 1], score[c % 2][:, 0:P * (c + 1)], AX.X,
                                   negate=True).then_inc(score_maxed.sem, 1)

                def attended(c):
                    dve.wait_ge(prob_ready.sem, prob_ready.at(b, c + 1))
                    dve.reciprocal(s_rsum[:, c:c + 1], s_sum[:, c:c + 1]).then_inc(prob_recip.sem, 1)
                    dve.wait_ge(rows_ready.sem, rows_ready.at(b, 3 * C + c + 1))
                    dve.wait_ge(prob_recip.sem, prob_recip.at(b, c + 1))
                    dve.scalar_tensor_tensor(x_res[:, c], rows[c % 2][:, 0:E], s_rsum[:, c:c + 1], x_res[:, c],
                                             ALU.mult, ALU.add).then_inc(rows_taken.sem, 1)

                score_max(0)
                for c in range(C):
                    if c + 1 < C:
                        score_max(c + 1)
                    n = P * (c + 1)
                    dve.wait_ge(probT_hi.sem, probT_hi.at(b, c + 1))
                    dve.tensor_tensor(probT[:, 1, c % 2, 0:n], turned[c % 2][:, 0:n], probT[:, 0, c % 2, 0:n],
                                      ALU.subtract).then_inc(probT_split.sem, 1)
                    if c:
                        attended(c - 1)
                attended(C - 1)
                dve.wait_ge(rows_taken.sem, rows_taken.at(b, 4 * C))
                layernorm(b, 2, x_res)
                turn(b, 3)
                dve.wait_ge(logit_ready.sem, logit_ready.at(b, 1))
                dve.tensor_copy(logit[:], turned[0][:, 0:C * NE].rearrange("p (c e) -> p c e", c=C))\
                   .then_inc(logit_copied.sem, 1)
                hold(dve, logit_copied, logit_copied.at(b, 1))
                for c in range(C):
                    last = dve.max(top[:, c], logit[:, c])
                last.then_inc(topped.sem, 1)
                hold(dve, topped, topped.at(b, 1))
                for c in range(C):
                    last = dve.max_index(top_i[:, c], top[:, c], logit[:, c])
                last.then_inc(top_found.sem, 1)
                dve.tensor_tensor(e2_in[:], top[:, :, 1], top[:, :, 0], ALU.subtract).then_inc(shifted.sem, 1)
                dve.tensor_tensor(l_shift[:], logit[:], top[:, :, 0:1].to_broadcast([P, C, NE]),
                                  ALU.subtract).then_inc(shifted.sem, 1)
                dve.wait_ge(top_found.sem, top_found.at(b, 1))
                dve.tensor_copy(top_f[:], top_i[:, :, 0:2]).then_inc(weigh.sem, 1)
                dve.wait_ge(l_exped.sem, l_exped.at(b, 2))
                dve.reduce_sum(l_sum[:], l_exp[:], AX.X).then_inc(weigh.sem, 1)
                dve.tensor_scalar(w_one[:], e2[:], 1.0, None, ALU.add).then_inc(weigh.sem, 1)
                dve.wait_ge(weigh.sem, weigh.at(b, 3))
                dve.scalar_tensor_tensor(w_den[:], l_sum[:], 1e-9, w_one[:], ALU.mult, ALU.add).then_inc(weigh.sem, 1)
                dve.wait_ge(weigh.sem, weigh.at(b, 4))
                dve.tensor_scalar(w_den2[:], w_den[:], 2.0, None, ALU.mult).then_inc(weigh.sem, 1)
                dve.wait_ge(weigh.sem, weigh.at(b, 5))
                dve.reciprocal(w_1[:], w_den2[:]).then_inc(weigh.sem, 1)
                dve.wait_ge(weigh.sem, weigh.at(b, 6))
                dve.tensor_tensor(w_2[:], w_1[:], e2[:], ALU.mult).then_inc(weigh.sem, 1)
                dve.wait_ge(weigh.sem, weigh.at(b, 7))
                for c in range(C):
                    dve.tensor_scalar(comb1[:, c], expert_no[:], top_f[:, c, 0:1], w_1[:, c:c + 1],
                                      ALU.is_equal, ALU.mult)
                    last = dve.tensor_scalar(comb2[:, c], expert_no[:], top_f[:, c, 1:2], w_2[:, c:c + 1],
                                             ALU.is_equal, ALU.mult)
                last.then_inc(weigh.sem, 1)
                dve.wait_ge(weigh.sem, weigh.at(b, 8))
                dve.tensor_tensor(comb[:], comb1[:], comb2[:], ALU.add).then_inc(weigh.sem, 1)
                dve.wait_ge(combT_ready.sem, combT_ready.at(b, 1))
                dve.tensor_copy(combT[:], turned[1][0:NE, :]).then_inc(combT_copied.sem, 1)

                def part_mid(j):
                    dve.wait_ge(mid_hi.sem, mid_hi.at(b, j + 1))
                    if j < NSH:
                        dve.scalar_tensor_tensor(mid[:, 1, j % 2], gtu[:, j % 2], 0.5, mid[:, 0, j % 2],
                                                 ALU.mult, ALU.subtract).then_inc(mid_split.sem, 1)
                    else:
                        dve.tensor_tensor(mid[:, 1, j % 2], midc[:, j % 2], mid[:, 0, j % 2],
                                          ALU.subtract).then_inc(mid_split.sem, 1)

                for j in range(MID):
                    dve.wait_ge(tanh_done.sem, tanh_done.at(b, j + 1))
                    dve.scalar_tensor_tensor(gt[:, j % 2], th[:, j % 2], 1.0, score[j % 2][:], ALU.add,
                                             ALU.mult).then_inc(gt_done.sem, 1)
                    dve.wait_ge(u_ready.sem, u_ready.at(b, j + 1))
                    dve.wait_ge(gt_done.sem, gt_done.at(b, j + 1))
                    dve.tensor_tensor(gtu[:, j % 2], gt[:, j % 2], rows[j % 2][:], ALU.mult).then_inc(gtu_done.sem, 1)
                    if j >= NSH:
                        dve.wait_ge(gtu_done.sem, gtu_done.at(b, j + 1))
                        dve.wait_ge(comb_ready.sem, comb_ready.at(b, j - NSH + 1))
                        dve.tensor_tensor(midc[:, j % 2], gtu[:, j % 2], turned[j % 2][:],
                                          ALU.mult).then_inc(midc_done.sem, 1)
                    if j:
                        part_mid(j - 1)
                part_mid(MID - 1)
                dve.wait_ge(y_ready.sem, y_ready.at(b, 1))
                for g in range(2):
                    last = dve.tensor_tensor(x_res[:, 2 * g:2 * g + 2], x_res[:, 2 * g:2 * g + 2],
                                             wide[:, g].rearrange("p (c e) -> p c e", c=2), ALU.add)
                last.then_inc(y_taken.sem, 1)

        @block.tensor
        def _(pe):
            pe.wait_ge(w_lo, FIRST_ROUND)
            for m in range(K2):
                for k in range(K2):
                    last = three_passes(pe, rows[m][:, 0:E], parts(w_gu, k, slice(P * m, P * m + P)),
                                        parts(w_gu, k, slice(E, 2 * E)), start=(k == 0), stop=(k == K2 - 1))
                last.then_inc(qk_product, 1)
            pe.wait_ge(const_made, 11)
            pe.wait_ge(w_lo, SPLITS)
            pe.sem_inc(turned_ready.sem, 1)
            pe.sem_inc(hT_used.sem, 1)
            pe.sem_inc(toep_used.sem, 1)
            pe.sem_inc(vals_used.sem, 1)
            pe.sem_inc(q_used.sem, 1)
            pe.sem_inc(c_used.sem, 1)
            pe.sem_inc(probT_ready.sem, 1)
            pe.sem_inc(probT_used.sem, 2)
            pe.sem_inc(mid_used.sem, 2)

            def turn(b, n, src):
                pe.wait_ge(hT_ready.sem, hT_ready.at(b, 2 * n))
                for k in range(K2):
                    for c in range(C):
                        last = pe.transpose(turned[k][:, P * c:P * c + P], src[:, c, P * k:P * k + P], ident[:])
                    last.then_inc(turned_ready.sem, 1)

            def project(out, w, c):
                for k in range(K2):
                    last = three_passes(pe, out, parts(hT, k, slice(P * c, P * c + P)), parts(w, k, slice(None)),
                                        start=(k == 0), stop=(k == K2 - 1))
                return last

            with pe.Fori(0, B) as b:
                pe.wait_ge(h_ready.sem, h_ready.at(b, 1))
                pe.wait_ge(midc_done.sem, midc_done.at(b, 0))
                turn(b, 0, h)
                pe.wait_ge(hT_ready.sem, hT_ready.at(b, 2))
                pe.wait_ge(gtu_done.sem, gtu_done.at(b, 0))
                for k in range(K2):
                    last = three_passes(pe, score[0][:], parts(w_a, k, slice(None)), parts(hT, k, slice(None)),
                                        start=(k == 0), stop=(k == K2 - 1))
                last.then_inc(z_ready.sem, 1)
                for c in range(C):
                    pe.wait_ge(rows_taken.sem, rows_taken.at(b, c - 1))
                    last = project(rows[c % 2][:, 0:E], w_v, c)
                    last.then_inc(rows_ready.sem, 1)
                    if c == C - 1:
                        pe.wait_ge(rows_ready.sem, rows_ready.at(b, C))
                        pe.sem_inc(hT_used.sem, 1)
                pe.wait_ge(c_split.sem, c_split.at(b, 1))
                for c in range(C):
                    pe.wait_ge(rows_taken.sem, rows_taken.at(b, C + c - 1))
                    for k in range(K2):
                        last = three_passes(pe, rows[c % 2][:, 0:E], parts(cT, k, slice(P * c, P * c + P)),
                                            parts(w_vx, k, slice(None)), start=(k == 0), stop=(k == K2 - 1))
                    last.then_inc(rows_ready.sem, 1)
                pe.wait_ge(y_taken.sem, y_taken.at(b, 0))
                for m in range(K2):
                    for k in range(K2):
                        last = three_passes(pe, wide[:, m], parts(w_qk, k, slice(P * m, P * m + P)),
                                            parts(cT, k, slice(None)), start=(k == 0), stop=(k == K2 - 1))
                    last.then_inc(q_ready.sem, 1)
                pe.wait_ge(q_split.sem, q_split.at(b, 2))
                pe.sem_inc(c_used.sem, 1)
                pe.wait_ge(rows_taken.sem, rows_taken.at(b, C))
                pe.wait_ge(toep_loaded.sem, toep_loaded.at(b, 32))
                for g in range(2):
                    for hh in range(8):
                        head = 8 * g + hh
                        acc = wide[:, g, C * D * hh:C * D * (hh + 1)].rearrange("p (c d) -> p c d", c=C)
                        for delta in range(C):
                            window = [toep[:, a, head, P * delta:P * delta + P] for a in range(2)]
                            keys = [val[:, a, head, 0:C - delta, :] for a in range(2)]
                            last = three_passes(pe, acc[:, delta:C, :], window, keys,
                                                start=(delta == 0), stop=(delta == C - 1), skip_group_check=True)
                    last.then_inc(mix_ready.sem, 1)
                pe.wait_ge(mix_ready.sem, mix_ready.at(b, 2))
                pe.sem_inc(toep_used.sem, 1)
                pe.sem_inc(vals_used.sem, 1)
                pe.wait_ge(mix_taken.sem, mix_taken.at(b, 2))
                turn(b, 1, mix)
                pe.wait_ge(hT_ready.sem, hT_ready.at(b, 4))
                for c in range(C):
                    pe.wait_ge(rows_taken.sem, rows_taken.at(b, 2 * C + c - 1))
                    project(rows[c % 2][:, 0:E], w_o, c).then_inc(rows_ready.sem, 1)
                pe.wait_ge(rows_ready.sem, rows_ready.at(b, 3 * C))
                pe.sem_inc(hT_used.sem, 1)
                pe.wait_ge(h_ready.sem, h_ready.at(b, 2))
                turn(b, 2, h)
                pe.wait_ge(hT_ready.sem, hT_ready.at(b, 6))
                pe.wait_ge(q_split.sem, q_split.at(b, 2))

                def scores(c):
                    n = P * (c + 1)
                    if c >= 2:
                        pe.wait_ge(prob_ready.sem, prob_ready.at(b, c - 1))
                    for k in range(K2):
                        three_passes(pe, score[c % 2][:, 0:n], parts(qT, k, slice(P * c, P * c + P)),
                                     parts(hT, k, slice(0, n)), start=(k == 0), stop=False, skip_group_check=True)
                    pe.matmul(score[c % 2][:, n - P:n], ident16[:], future[:], start=False, stop=True,
                              skip_group_check=True).then_inc(score_ready.sem, 1)

                def turn_probs(c):
                    pe.wait_ge(prob_ready.sem, prob_ready.at(b, c + 1))
                    pe.wait_ge(probT_split.sem, probT_split.at(b, max(c - 1, 0)))
                    for t in range(c + 1):
                        last = pe.transpose(turned[c % 2][:, P * t:P * t + P], prob[:, c % 2, P * t:P * t + P], ident[:])
                    last.then_inc(probT_ready.sem, 1)

                def attend(c):
                    pe.wait_ge(probT_split.sem, probT_split.at(b, c + 1))
                    pe.wait_ge(rows_taken.sem, rows_taken.at(b, 3 * C + c - 1))
                    for t in range(c + 1):
                        last = three_passes(pe, rows[c % 2][:, 0:E], parts(probT, c % 2, slice(P * t, P * t + P)),
                                            parts(vx, t, slice(None)), start=(t == 0), stop=(t == c))
                    last.then_inc(rows_ready.sem, 1)
                    pe.wait_ge(rows_ready.sem, rows_ready.at(b, 3 * C + c + 1))
                    pe.sem_inc(probT_used.sem, 1)

                scores(0)
                for c in range(C):
                    if c + 1 < C:
                        scores(c + 1)
                    turn_probs(c)
                    if c:
                        attend(c - 1)
                attend(C - 1)
                pe.sem_inc(hT_used.sem, 1)
                pe.sem_inc(q_used.sem, 1)
                pe.wait_ge(h_ready.sem, h_ready.at(b, 3))
                pe.wait_ge(probT_split.sem, probT_split.at(b, 4))
                turn(b, 3, h)
                pe.wait_ge(hT_ready.sem, hT_ready.at(b, 8))
                for c in range(C):
                    for k in range(K2):
                        last = three_passes(pe, turned[0][:, NE * c:NE * c + NE], parts(hT, k, slice(P * c, P * c + P)),
                                            parts(w_r, k, slice(None)), start=(k == 0), stop=(k == K2 - 1))
                last.then_inc(logit_ready.sem, 1)

                def combine():
                    pe.wait_ge(weigh.sem, weigh.at(b, 9))
                    for c in range(C):
                        last = pe.transpose(turned[1][0:NE, P * c:P * c + P], comb[:, c], ident[:])
                    last.then_inc(combT_ready.sem, 1)

                def gate_up(j):
                    if j >= 2:
                        pe.wait_ge(gtu_done.sem, gtu_done.at(b, j - 1))
                    for at, bank_, ready in ((0, score[j % 2], g_ready), (P, rows[j % 2], u_ready)):
                        for k in range(K2):
                            last = three_passes(pe, bank_[:], parts(w_gu, k, slice(2 * P * j + at, 2 * P * j + at + P)),
                                                parts(hT, k, slice(None)), start=(k == 0), stop=(k == K2 - 1))
                        last.then_inc(ready.sem, 1)
                    if j >= NSH:
                        if j == NSH:
                            pe.wait_ge(combT_copied.sem, combT_copied.at(b, 1))
                        if j >= NSH + 2:
                            pe.wait_ge(midc_done.sem, midc_done.at(b, j - NSH - 1))
                        pe.matmul(turned[j % 2][:], spread[:, j - NSH, :], combT[:], start=True,
                                  stop=True).then_inc(comb_ready.sem, 1)

                def down(j):
                    pe.wait_ge(mid_split.sem, mid_split.at(b, j + 1))
                    for c in range(C):
                        last = three_passes(pe, wide[:, c // 2, E * (c % 2):E * (c % 2) + E],
                                            parts(mid, j % 2, slice(P * c, P * c + P)), parts(w_d, j, slice(None)),
                                            start=(j == 0 and c % 2 == 0), stop=(j == MID - 1), skip_group_check=True)
                    last.then_inc(mid_used.sem, 1)

                pe.wait_ge(rows_taken.sem, rows_taken.at(b, 4 * C))
                for j in range(MID):
                    gate_up(j)
                    if j == 1:
                        combine()
                    if j:
                        down(j - 1)
                down(MID - 1)
                pe.wait_ge(mid_used.sem, mid_used.at(b, MID))
                pe.sem_inc(y_ready.sem, 1)
                pe.sem_inc(hT_used.sem, 1)


def kernel(x, ctx_1024, L0_attn_W_A, L0_attn_W_V, L0_attn_W_O, L0_attn_b_O, L0_xattn_WK, L0_xattn_WV,
           L0_xattn_WQ, L0_ffn_router_w, L0_ffn_wg_r, L0_ffn_wu_r, L0_ffn_wd_r, L0_ffn_wg_s, L0_ffn_wu_s,
           L0_ffn_wd_s):
    import numpy as np
    import concourse.bacc as bacc
    from concourse.bass_utils import run_bass_kernel_spmd

    def gate_up_columns(g, u):
        n, d, m = g.shape
        g, u = (np.transpose(np.asarray(w), (1, 0, 2)).reshape(d, n * m // P, 1, P) for w in (g, u))
        return np.ascontiguousarray(np.concatenate([g, u], axis=2).reshape(d, 2 * n * m))

    arrays = {
        "x": np.asarray(x),
        "ctxT": np.ascontiguousarray(np.transpose(np.asarray(ctx_1024), (0, 2, 1))),
        "wa": np.ascontiguousarray(np.asarray(L0_attn_W_A).T),
        "wv": np.ascontiguousarray(np.asarray(L0_attn_W_V).T),
        "wo": np.ascontiguousarray(np.asarray(L0_attn_W_O).T),
        "bo": np.asarray(L0_attn_b_O),
        "wq": np.ascontiguousarray(np.asarray(L0_xattn_WQ).T),
        "wk": np.ascontiguousarray(np.asarray(L0_xattn_WK).T),
        "wvx": np.asarray(L0_xattn_WV),
        "rw": np.asarray(L0_ffn_router_w),
        "gu_s": gate_up_columns(L0_ffn_wg_s, L0_ffn_wu_s),
        "wd_s": np.asarray(L0_ffn_wd_s).reshape(-1, E),
        "gu_r": gate_up_columns(L0_ffn_wg_r, L0_ffn_wu_r),
        "wd_r": np.asarray(L0_ffn_wd_r).reshape(-1, E),
    }
    nc = bacc.Bacc("TRN2", target_bir_lowering=False, num_devices=1)
    args = [nc.dram_tensor(f"in_{n}", a.shape, mybir.dt.from_np(a.dtype), kind="ExternalInput").ap()
            for n, a in arrays.items()]
    out = nc.dram_tensor("out_0", (B, S, E), F32, kind="ExternalOutput").ap()
    decoder_layer(nc, *args, out)
    r = run_bass_kernel_spmd(nc, [{f"in_{n}": a for n, a in arrays.items()}], core_ids=[0])
    return r.results[0]["out_0"]
```

```python
from contextlib import ExitStack

import concourse.bass as bass
from concourse import mybir

P = 128
ALU = mybir.AluOpType
ACT = mybir.ActivationFunctionType
AX = mybir.AxisListType
F32 = mybir.dt.float32
F16 = mybir.dt.float16
BF16 = mybir.dt.bfloat16
U32 = mybir.dt.uint32
I32 = mybir.dt.int32

B, S, E = 8, 512, 256
H, D = 16, 16
NE, MR = 16, 64
C = S // P
K2 = E // P
NSH = 2
PAIRS = NE * MR // P
MID = NSH + PAIRS
PAD = P
ZROW = PAD + S
EPS = 1e-5
NEG = -1e30
SLOTS = 3

X_H = 256.0
X_W = 64.0
X_Z = 4096.0
X_V = 16.0
X_MIX = 64.0
X_QK = 1024.0
X_Q = 256.0
X_VX = 16.0
X_P = 4096.0
X_COMB = 512.0
X_MID = 16.0

TURNED = (["h3.0", "h3.1", "h1.0", "h1.1", "mix.0", "mix.1", "h2.0", "h2.1", "combT"]
          + ["cb2", "pt0", "cb3", "pt1", "cb4", "pt2", "cb5", "pt3", "cb6", "cb7", "cb8", "cb9", "none"])
SCORE = ["z", "g0", "g1", "s0", "s1", "g2", "s2", "g3", "s3", "g4", "g5", "g6", "g7", "g8", "g9", "none"]
ROWS = (["v0", "v1", "v2", "v3", "logit", "x0", "x1", "o0", "o1", "o2", "o3", "x2", "x3", "u0", "u1", "u2", "u3"]
        + ["p0", "u4", "p1", "u5", "p2", "u6", "p3", "u7", "u8", "u9", "none"])


class Signal:

    def __init__(self, sem, per_round, before=0):
        self.sem, self.per_round, self.before = sem, per_round, before

    def at(self, n, count):
        return n * self.per_round + (count + self.before)


class Banks:

    def __init__(self, order, banks, ready, taken):
        assert len(order) % 2 == 0
        self.order, self.banks = order, banks
        n = len(order)
        self.ready, self.taken = Signal(ready, n, n), Signal(taken, n, n)

    def bank(self, use):
        return self.banks[self.order.index(use) % 2]

    def is_ready(self, it, use):
        return self.ready.at(it, self.order.index(use) + 1)

    def was_ready(self, it, use):
        return self.ready.at(it, self.order.index(use) + 1 - len(self.order))

    def is_taken(self, it, use):
        return self.taken.at(it, self.order.index(use) + 1)

    def is_free(self, it, use):
        return self.taken.at(it, self.order.index(use) - 1)

    def skip(self, eng, signal, it, *uses):
        at = self.order.index(uses[0])
        eng.wait_ge(signal.sem, signal.at(it, at))
        eng.sem_inc(signal.sem, len(uses))


def three_passes(pe, out, stationary, moving, start, stop, **kw):
    pe.matmul(out, stationary[0], moving[0], start=start, stop=False, **kw)
    pe.matmul(out, stationary[0], moving[1], start=False, stop=False, **kw)
    return pe.matmul(out, stationary[1], moving[0], start=False, stop=stop, **kw)


def decoder_layer(nc, x, ctxT, wa, wv, wo, bo, wq, wk, wvx, rw, gu_s, wd_s, gu_r, wd_r, out):
    with ExitStack() as ctx:
        def sb(name, shape, dt=F32):
            return ctx.enter_context(nc.sbuf_tensor(name, shape, dt))

        def bank(name, shape=(P, 512), dt=F32):
            return ctx.enter_context(nc.psum_tensor(name, list(shape), dt))

        def sem(name):
            return ctx.enter_context(nc.semaphore(name))

        def sig(name, per_batch, before=0):
            return Signal(sem(name), per_batch, before)

        w_a = sb("w_a", [P, 2, K2, H], F16)
        w_v = sb("w_v", [P, 2, K2, E], F16)
        w_o = sb("w_o", [P, 2, K2, E], F16)
        w_q = sb("w_q", [P, 2, K2, E], F16)
        w_k = sb("w_k", [P, 2, K2, E], F16)
        w_qk = sb("w_qk", [P, 2, K2, E], F16)
        w_vx = sb("w_vx", [P, 2, K2, E], F16)
        w_r = sb("w_r", [P, 2, K2, NE], F16)
        w_gu = sb("w_gu", [P, 2, K2, 2 * MID * P], F16)
        w_d = sb("w_d", [P, 2, MID, E], F16)
        NS, NR = 2 * NSH * P, 2 * PAIRS * P

        ident = sb("ident", [P, P])
        ident16 = sb("ident16", [P, P], BF16)
        future = sb("future", [P, P], BF16)
        expert_no_i = sb("expert_no_i", [P, NE], I32)
        expert_no = sb("expert_no", [P, NE])
        spread = sb("spread", [NE, PAIRS, P], F16)
        zeros16 = sb("zeros16", [2 * H, PAD], F16)
        minus_half = sb("minus_half", [P, C])
        b_o = sb("b_o", [P, E])

        x_in = sb("x_in", [P, C, E])
        x_bo = sb("x_bo", [P, C, E])
        h1 = sb("h1", [P, C, E])
        h1T = sb("h1T", [P, 2, K2, S], F16)
        z_nmax = sb("z_nmax", [H, 1])
        z_bias = sb("z_bias", [H, 1])
        z_exp = sb("z_exp", [H, S])
        z_sum = sb("z_sum", [H, 1])
        z_rsum = sb("z_rsum", [H, 1])
        z_norm = sb("z_norm", [H, S])
        z_parts = sb("z_parts", [H, 2, S], F16)
        toep = sb("toep", [P, 2, H, S], F16)
        val = sb("val", [P, 2, H, C, D], F16)
        cT_in = sb("cT_in", [P, K2, S])
        cT = sb("cT", [P, 2, K2, S], F16)

        mix = sb("mix", [P, C, E])
        mixT = sb("mixT", [P, 2, K2, S], F16)
        vx = sb("vx", [P, 2, C, E], F16)
        qT = sb("qT", [P, 2, K2, S], F16)
        x_res = sb("x_res", [P, C, E])
        h2 = sb("h2", [P, C, E])
        h2T = sb("h2T", [P, 2, K2, S], F16)
        s_nmax = sb("s_nmax", [P, C])
        s_bias = sb("s_bias", [P, C])
        s_sum = sb("s_sum", [P, C])
        s_scaled = sb("s_scaled", [P, C])
        s_rsum = sb("s_rsum", [P, C])
        prob = sb("prob", [P, 2, S])
        probT = sb("probT", [P, 2, 2, S], F16)
        h3 = sb("h3", [P, C, E])

        x_out = sb("x_out", [P, C, E])
        h3T = sb("h3T", [P, 2, K2, S], F16)
        logit = sb("logit", [P, C, NE])
        top = sb("top", [P, C, 8])
        top_i = sb("top_i", [P, C, 8], U32)
        top_f = sb("top_f", [P, C, 2])
        l_shift = sb("l_shift", [P, C, NE])
        l_exp = sb("l_exp", [P, C, NE])
        e2_in = sb("e2_in", [P, C])
        e2 = sb("e2", [P, C])
        l_sum = sb("l_sum", [P, C])
        w_one = sb("w_one", [P, C])
        w_den = sb("w_den", [P, C])
        w_scaled = sb("w_scaled", [P, C])
        w_1 = sb("w_1", [P, C])
        w_2 = sb("w_2", [P, C])
        comb1 = sb("comb1", [P, C, NE])
        comb2 = sb("comb2", [P, C, NE])
        comb = sb("comb", [P, C, NE])
        combT = sb("combT", [NE, 2, S], F16)
        gated = sb("gated", [P, SLOTS, S])
        mid = sb("mid", [P, 2, SLOTS, S], F16)

        stats = [sb(f"stats{n}", [P, C, 6]) for n in range(3)]
        mean_var = [sb(f"mean_var{n}", [P, C, 2]) for n in range(3)]
        var_eps = [sb(f"var_eps{n}", [P, C]) for n in range(3)]
        rstd = [sb(f"rstd{n}", [P, C]) for n in range(3)]

        loads = [
            ("wa", wa, w_a, K2, H),
            ("wv", wv, w_v, K2, E),
            ("wq", wq, w_q, K2, E),
            ("wk", wk, w_k, K2, E),
            ("wvx", wvx, w_vx, K2, E),
            ("wo", wo, w_o, K2, E),
            ("rw", rw, w_r, K2, NE),
            ("gu_s", gu_s, w_gu[:, :, :, 0:NS], K2, NS),
            ("wd_s", wd_s, w_d[:, :, 0:NSH], NSH, E),
            ("gu_r", gu_r, w_gu[:, :, :, NS:NS + NR], K2, NR),
            ("wd_r", wd_r, w_d[:, :, NSH:MID], PAIRS, E),
        ]
        EARLY = [n for n, *_ in loads].index("wk") + 1
        borrowed = {"gu_s": (x_out, 0), "wd_s": (h3, 0), "wo": (h3, 2), "wvx": (x_res, 0)}
        stage = sb("stage", [P, sum(k * n for name, _, _, k, n in loads if name not in borrowed)])
        staged, at = {}, 0
        for name, _, _, k, n in loads:
            if name in borrowed:
                buffer, c = borrowed[name]
                flat = buffer[:, c:c + k * n // E].rearrange("p c e -> p (c e)")
            else:
                flat = stage[:, at:at + k * n]
                at += k * n
            staged[name] = flat.rearrange("p (k n) -> p k n", k=k)

        turned = Banks(TURNED, [bank(f"turned{k}") for k in range(2)], sem("turned_ready"), sem("turned_taken"))
        score = Banks(SCORE, [bank(f"score{k}") for k in range(2)], sem("score_ready"), sem("score_taken"))
        rows = Banks(ROWS, [bank(f"rows{k}") for k in range(2)], sem("rows_ready"), sem("rows_taken"))
        wide = bank("wide", [P, 2, 512])

        z_dram = nc.dram_tensor("z_scratch", [B, 2 * H, ZROW], F16, kind="Internal").ap()

        w_loaded = [sem(f"loaded_{n}") for n, *_ in loads]
        w_hi = sem("w_hi")
        w_lo = sem("w_lo")
        qk_product = sem("qk_product")
        qk_hi = sem("qk_hi")
        qk_lo = sem("qk_lo")
        const_made = sem("const_made")
        pads_stored = sem("pads_stored")
        bo_loaded = sem("bo_loaded")
        held = {eng.engine: sem(f"held_{n}") for n, eng in (("dve", nc.vector), ("pool", nc.gpsimd))}

        x_loaded = sig("x_loaded", 16)
        c_loaded = sig("c_loaded", 16)
        z_stored = sig("z_stored", 16)
        toep_loaded = sig("toep_loaded", 32)
        y_stored = sig("y_stored", 16, 16)
        stats_done = [sig(f"stats_done{n}", 1) for n in range(3)]
        aggr_done = [sig(f"aggr_done{n}", 1) for n in range(3)]
        eps_added = [sig(f"eps_added{n}", 1) for n in range(3)]
        rstd_done = [sig(f"rstd_done{n}", 1) for n in range(3)]
        h_ready = [sig(f"h_ready{n}", 1, 1) for n in range(3)]
        x_biased = sig("x_biased", 1, 1)
        c_hi = sig("c_hi", 1)
        c_split = sig("c_split", 1, 1)
        h1T_hi = sig("h1T_hi", 2)
        h2T_hi = sig("h2T_hi", 2)
        h3T_hi = sig("h3T_hi", 2)
        mixT_hi = sig("mixT_hi", 2)
        z_maxed = sig("z_maxed", 2)
        z_exped = sig("z_exped", 1)
        z_scaled = sig("z_scaled", 2)
        z_split = sig("z_split", 1)
        val_hi = sig("val_hi", C)
        vx_hi = sig("vx_hi", C)
        mix_ready = sig("mix_ready", 2)
        mix_taken = sig("mix_taken", 2, 2)
        q_ready = sig("q_ready", 2, 2)
        q_hi = sig("q_hi", 2)
        q_split = sig("q_split", 2, 2)
        row_max = sig("row_max", C)
        score_maxed = sig("score_maxed", C)
        prob_ready = sig("prob_ready", C)
        prob_scaled = sig("prob_scaled", C)
        probT_hi = sig("probT_hi", C)
        x_kept = sig("x_kept", 1, 1)
        logit_copied = sig("logit_copied", 1)
        topped = sig("topped", 1)
        top_found = sig("top_found", 1)
        shifted = sig("shifted", 2)
        l_exped = sig("l_exped", 2)
        weighed = sig("weighed", 9)
        combT_hi = sig("combT_hi", 1)
        tanh_done = sig("tanh_done", MID)
        gated_done = sig("gated_done", NSH)
        comb_done = sig("comb_done", PAIRS)
        mid_hi = sig("mid_hi", MID)
        mid_split = sig("mid_split", MID, MID)
        y_ready = sig("y_ready", 1)
        y_taken = sig("y_taken", 1, 2)

        def hold(eng, signal, value):
            eng.wait_ge(signal.sem, value)
            eng.sem_inc(held[eng.engine], 1)

        def backwards(row):
            return row.rearrange("p (c t) -> p c t", t=P)[:, :, ::-1]

        def parts(t, *index):
            return [t[(slice(None), a, *index)] for a in range(2)]

        def iterations(eng, iteration):
            iteration(0, True, False, False)
            iteration(1, True, True, False)
            with eng.Fori(2, B) as it:
                iteration(it, True, True, True)
            iteration(B, False, True, True)
            iteration(B + 1, False, False, True)

        block = ctx.enter_context(nc.Block())

        @block.sync
        def _(sp):
            def load_x(b):
                sp.wait_ge(h_ready[0].sem, h_ready[0].at(b, 0))
                sp.wait_ge(x_biased.sem, x_biased.at(b, 0))
                sp.dma_start(x_in[:], x[b].rearrange("(c p) e -> p c e", p=P)).then_inc(x_loaded.sem, 16)

            def load_context(b):
                sp.wait_ge(c_split.sem, c_split.at(b, 0))
                sp.dma_start(cT_in[:], ctxT[b].rearrange("(k p) s -> p k s", p=P)).then_inc(c_loaded.sem, 16)

            load_x(0)
            for n, (name, src, _, _, _) in enumerate(loads):
                sp.dma_start(staged[name], src.rearrange("(k p) n -> p k n", p=P)).then_inc(w_loaded[n], 16)
                if name == "wk":
                    sp.dma_start(b_o[:], bo.partition_broadcast(P)).then_inc(bo_loaded, 16)
                    load_context(0)
            sp.wait_ge(const_made, 1)
            for b in range(B):
                sp.dma_start(z_dram[b, :, 0:PAD], zeros16[:]).then_inc(pads_stored, 16)
            sp.wait_ge(pads_stored, 16 * B)

            def iteration(it, f, m, d, last_f=False):
                if f:
                    sp.wait_ge(z_split.sem, z_split.at(it, 1))
                    sp.dma_start(z_dram[it, :, PAD:ZROW].rearrange("(a h) s -> h a s", a=2),
                                 z_parts[:]).then_inc(z_stored.sem, 16)
                    sp.wait_ge(z_stored.sem, z_stored.at(it, 16))
                    for a in range(2):
                        src = z_dram[it, a * H:(a + 1) * H, PAD - P + 1:ZROW]
                        skewed = bass.AP(src.tensor, src.offset, [[1, P], [ZROW, H], [1, S]])
                        sp.dma_start(toep[:, a], skewed).then_inc(toep_loaded.sem, 16)
                    if not last_f:
                        load_x(it + 1)
                        load_context(it + 1)
                if d:
                    sp.wait_ge(y_taken.sem, y_taken.at(it - 2, 1))
                    sp.dma_start(out[it - 2].rearrange("(c p) e -> p c e", p=P), x_out[:]).then_inc(y_stored.sem, 16)

            iteration(0, True, False, False)
            iteration(1, True, True, False)
            with sp.Fori(2, B - 1) as it:
                iteration(it, True, True, True)
            iteration(B - 1, True, True, True, last_f=True)
            iteration(B, False, True, True)
            iteration(B + 1, False, False, True)
            sp.wait_ge(y_stored.sem, y_stored.at(B, 0))

        @block.gpsimd
        def _(pool):
            pool.memset(zeros16[:], 0.0).then_inc(const_made, 1)
            pool.memset(ident[:], 0.0).then_inc(const_made, 1)
            pool.memset(future[:], 0.0).then_inc(const_made, 1)
            pool.memset(spread[:], 0.0).then_inc(const_made, 1)
            pool.memset(minus_half[:], -0.5).then_inc(const_made, 1)
            pool.iota(expert_no_i[:], pattern=[[1, NE]], base=0, channel_multiplier=0).then_inc(const_made, 1)
            pool.wait_ge(const_made, 6)
            pool.affine_select(out=ident[:], in_=ident[:], compare_op=ALU.not_equal, fill=1.0, base=0,
                               pattern=[[-1, P]], channel_multiplier=1).then_inc(const_made, 1)
            pool.affine_select(out=future[:], in_=future[:], compare_op=ALU.is_ge, fill=NEG, base=0,
                               pattern=[[-1, P]], channel_multiplier=1).then_inc(const_made, 1)
            spread4 = spread[:].rearrange("e q (g m) -> e q g m", g=2)
            pool.affine_select(out=spread4, in_=spread4, compare_op=ALU.not_equal, fill=1.0, base=0,
                               pattern=[[-2, PAIRS], [-1, 2], [0, MR]], channel_multiplier=1).then_inc(const_made, 1)
            pool.tensor_copy(expert_no[:], expert_no_i[:]).then_inc(const_made, 1)
            pool.wait_ge(const_made, 10)
            pool.tensor_copy(ident16[:], ident[:]).then_inc(const_made, 1)
            pool.sem_inc(x_biased.sem, 1)
            pool.sem_inc(c_split.sem, 1)
            pool.sem_inc(x_kept.sem, 1)
            pool.sem_inc(mid_split.sem, MID)
            pool.wait_ge(bo_loaded, 16)

            def reciprocal_deviation(b, n):
                hold(pool, aggr_done[n], aggr_done[n].at(b, 1))
                pool.tensor_scalar(var_eps[n][:], mean_var[n][:, :, 1], EPS, X_H ** -2, ALU.add,
                                   ALU.mult).then_inc(eps_added[n].sem, 1)
                pool.wait_ge(eps_added[n].sem, eps_added[n].at(b, 1))
                pool.tensor_tensor(rstd[n][:], var_eps[n][:], minus_half[:], ALU.pow).then_inc(rstd_done[n].sem, 1)

            def part_mid(b, j):
                pool.wait_ge(mid_hi.sem, mid_hi.at(b, j + 1))
                pool.tensor_tensor(mid[:, 1, j % SLOTS], gated[:, j % SLOTS], mid[:, 0, j % SLOTS],
                                   ALU.subtract).then_inc(mid_split.sem, 1)

            def iteration(it, f, m, d):
                if f:
                    reciprocal_deviation(it, 0)
                if d:
                    pool.wait_ge(h_ready[2].sem, h_ready[2].at(it - 2, 1))
                    hold(pool, y_stored, y_stored.at(it - 2, 0))
                    pool.tensor_copy(x_out[:], x_res[:]).then_inc(x_kept.sem, 1)
                if f:
                    if it is not 0:
                        pool.wait_ge(z_stored.sem, z_stored.at(it, 0))
                    hold(pool, score.taken, score.is_taken(it, "z"))
                    pool.tensor_scalar(z_norm[:], z_exp[:], z_rsum[:], X_Z, ALU.mult, ALU.mult)\
                        .then_inc(z_scaled.sem, 1)
                    hold(pool, z_scaled, z_scaled.at(it, 1))
                    pool.tensor_copy(z_parts[:, 0], z_norm[:]).then_inc(z_scaled.sem, 1)
                    pool.wait_ge(z_scaled.sem, z_scaled.at(it, 2))
                    pool.tensor_tensor(z_parts[:, 1], z_norm[:], z_parts[:, 0], ALU.subtract).then_inc(z_split.sem, 1)
                    pool.wait_ge(rows.taken.sem, rows.is_taken(it, "o3"))
                    for c in range(C):
                        last = pool.tensor_tensor(x_bo[:, c], x_in[:, c], b_o[:], ALU.add)
                    last.then_inc(x_biased.sem, 1)
                if m:
                    reciprocal_deviation(it - 1, 1)
                for j in range(6 if d else 0):
                    part_mid(it - 2, j)
                if m:
                    reciprocal_deviation(it - 1, 2)
                if f:
                    pool.wait_ge(c_loaded.sem, c_loaded.at(it, 16))
                    hold(pool, q_ready, q_ready.at(it, 0))
                    pool.tensor_copy(cT[:, 0], cT_in[:]).then_inc(c_hi.sem, 1)
                    pool.wait_ge(c_hi.sem, c_hi.at(it, 1))
                    pool.tensor_tensor(cT[:, 1], cT_in[:], cT[:, 0], ALU.subtract).then_inc(c_split.sem, 1)
                for j in range(6, MID if d else 0):
                    part_mid(it - 2, j)

            iterations(pool, iteration)

        @block.scalar
        def _(act):
            act.sem_inc(mix_taken.sem, 2)
            act.sem_inc(y_stored.sem, 16)

            def part_weights(some):
                for n in some:
                    name, _, dst, _, _ = loads[n]
                    act.wait_ge(w_loaded[n], 16)
                    act.activation(dst[:, 0], staged[name], ACT.Copy, scale=X_W).then_inc(w_hi, 1)

            def part_product():
                for k in range(K2):
                    act.wait_ge(qk_product, k + 1)
                    act.activation(w_qk[:, 0, k], wide[:, k, 0:E], ACT.Copy,
                                   scale=X_QK / (X_W * X_W * 16)).then_inc(qk_hi, 1)

            def part_turned(it, b, dst, hi, use, scale=1.0, reverse=False):
                for k in range(K2):
                    act.wait_ge(turned.ready.sem, turned.is_ready(it, f"{use}.{k}"))
                    src = turned.bank(f"{use}.{k}")[:]
                    act.activation(dst[:, 0, k], backwards(src) if reverse else src, ACT.Copy,
                                   scale=scale).then_inc(hi.sem, 1)

            def take_mix(b, g):
                act.wait_ge(mix_ready.sem, mix_ready.at(b, g + 1))
                act.activation(mix[:, :, P * g:P * g + P].rearrange("p c (h d) -> p h c d", d=D),
                               wide[:, g].rearrange("p (h c d) -> p h c d", c=C, d=D),
                               ACT.Copy, scale=X_MIX / (X_Z * X_V)).then_inc(mix_taken.sem, 1)

            def part_context(it, b, c):
                act.wait_ge(rows.ready.sem, rows.is_ready(it, f"x{c}"))
                act.activation(vx[:, 0, c], rows.bank(f"x{c}")[:, 0:E], ACT.Copy,
                               scale=X_VX / X_W).then_inc(vx_hi.sem, 1)

            def exp_scores(it, b, c):
                act.wait_ge(score_maxed.sem, score_maxed.at(b, c + 1))
                n = P * (c + 1)
                act.activation(prob[:, c % 2, 0:n], score.bank(f"s{c}")[:, 0:n], ACT.Exp, bias=s_bias[:, c:c + 1],
                               scale=1 / (X_Q * X_H), accum_out=s_sum[:, c:c + 1]).then_inc(prob_ready.sem, 1)

            def part_prob(it, b, c):
                act.wait_ge(turned.ready.sem, turned.is_ready(it, f"pt{c}"))
                n = P * (c + 1)
                act.activation(probT[:, 0, c % 2, 0:n], turned.bank(f"pt{c}")[:, 0:n], ACT.Copy,
                               scale=X_P).then_inc(probT_hi.sem, 1)

            def tanh(it, b, j):
                act.wait_ge(mid_split.sem, mid_split.at(b, j + 1 - SLOTS))
                act.wait_ge(score.ready.sem, score.is_ready(it, f"g{j}"))
                act.activation(gated[:, j % SLOTS], score.bank(f"g{j}")[:], ACT.Tanh,
                               scale=0.5 / (X_H * X_W)).then_inc(tanh_done.sem, 1)

            def part_mid(b, j):
                if j < NSH:
                    act.wait_ge(gated_done.sem, gated_done.at(b, j + 1))
                else:
                    act.wait_ge(comb_done.sem, comb_done.at(b, j - NSH + 1))
                act.activation(mid[:, 0, j % SLOTS], gated[:, j % SLOTS], ACT.Copy).then_inc(mid_hi.sem, 1)

            def iteration(it, f, m, d):
                if m:
                    take_mix(it - 1, 0)
                if d:
                    part_turned(it, it - 2, h3T, h3T_hi, "h3")
                if f:
                    part_turned(it, it, h1T, h1T_hi, "h1", reverse=True)
                if m:
                    take_mix(it - 1, 1)
                if f:
                    act.wait_ge(z_maxed.sem, z_maxed.at(it, 2))
                    act.activation(z_exp[:], backwards(score.bank("z")[0:H, :]), ACT.Exp, bias=z_bias[:],
                                   scale=D ** -0.5 / (X_H * X_W), accum_out=z_sum[:]).then_inc(z_exped.sem, 1)
                    for c in range(C):
                        act.wait_ge(rows.ready.sem, rows.is_ready(it, f"v{c}"))
                        act.activation(val[:, 0, :, c], rows.bank(f"v{c}")[:, 0:E].rearrange("p (h d) -> p h d", h=H),
                                       ACT.Copy, scale=X_V / (X_H * X_W)).then_inc(val_hi.sem, 1)
                if m:
                    part_turned(it, it - 1, mixT, mixT_hi, "mix")
                    for c in range(C):
                        part_context(it, it - 1, c)
                    for k in range(K2):
                        act.wait_ge(q_ready.sem, q_ready.at(it - 1, k + 1))
                        act.activation(qT[:, 0, k], wide[:, k], ACT.Copy, scale=X_Q / X_QK).then_inc(q_hi.sem, 1)
                if d:
                    tanh(it, it - 2, 0)
                if m:
                    part_turned(it, it - 1, h2T, h2T_hi, "h2")
                if d:
                    act.wait_ge(shifted.sem, shifted.at(it - 2, 2))
                    act.activation(e2[:], e2_in[:], ACT.Exp).then_inc(l_exped.sem, 1)
                    act.activation(l_exp[:], l_shift[:], ACT.Exp).then_inc(l_exped.sem, 1)
                    tanh(it, it - 2, 1)
                    part_mid(it - 2, 0)
                if m:
                    exp_scores(it, it - 1, 0)
                    exp_scores(it, it - 1, 1)
                for c in range(C):
                    if d:
                        tanh(it, it - 2, c + 2)
                        part_mid(it - 2, c + 1)
                    if m:
                        part_prob(it, it - 1, c)
                        if c < 2:
                            exp_scores(it, it - 1, c + 2)
                if d:
                    for j in range(6, MID):
                        tanh(it, it - 2, j)
                        part_mid(it - 2, j - 1)
                    part_mid(it - 2, MID - 1)

            early, late = range(EARLY), range(EARLY, len(loads))
            part_weights(early)
            iteration(0, True, False, False)
            part_product()
            part_weights(late)
            iteration(1, True, True, False)
            with act.Fori(2, B) as it:
                iteration(it, True, True, True)
            iteration(B, False, True, True)
            iteration(B + 1, False, False, True)

        @block.vector
        def _(dve):
            for banks in (turned, score, rows):
                dve.sem_inc(banks.taken.sem, len(banks.order))
            for n in range(3):
                dve.sem_inc(h_ready[n].sem, 1)
            dve.sem_inc(q_split.sem, 2)
            dve.sem_inc(y_taken.sem, 2)

            def part_weights(some):
                for n in some:
                    name, _, dst, _, _ = loads[n]
                    dve.wait_ge(w_hi, n + 1)
                    dve.scalar_tensor_tensor(dst[:, 1], staged[name], X_W, dst[:, 0], ALU.mult,
                                             ALU.subtract).then_inc(w_lo, 1)

            def part_product():
                for k in range(K2):
                    dve.wait_ge(qk_hi, k + 1)
                    dve.scalar_tensor_tensor(w_qk[:, 1, k], wide[:, k, 0:E], X_QK / (X_W * X_W * 16), w_qk[:, 0, k],
                                             ALU.mult, ALU.subtract).then_inc(qk_lo, 1)

            def statistics(b, n, src):
                for c in range(C):
                    last = dve.bn_stats(stats[n][:, c], src[:, c])
                last.then_inc(stats_done[n].sem, 1)
                hold(dve, stats_done[n], stats_done[n].at(b, 1))
                for c in range(C):
                    last = dve.bn_aggr(mean_var[n][:, c], stats[n][:, c])
                last.then_inc(aggr_done[n].sem, 1)

            def normalise(b, it, n, src, dst):
                dve.wait_ge(turned.ready.sem, turned.was_ready(it + (n == 2), f"h{n + 1}.1"))
                dve.wait_ge(rstd_done[n].sem, rstd_done[n].at(b, 1))
                for c in range(C):
                    last = dve.tensor_scalar(dst[:, c], src[:, c], mean_var[n][:, c, 0:1], rstd[n][:, c:c + 1],
                                             ALU.subtract, ALU.mult)
                last.then_inc(h_ready[n].sem, 1)

            def part_turned(b, dst, hi, use, reverse=False):
                for k in range(K2):
                    dve.wait_ge(hi.sem, hi.at(b, k + 1))
                    src = turned.bank(f"{use}.{k}")[:]
                    dve.tensor_tensor(dst[:, 1, k], backwards(src) if reverse else src, dst[:, 0, k],
                                      ALU.subtract).then_inc(turned.taken.sem, 1)

            def part_context(b, c):
                dve.wait_ge(vx_hi.sem, vx_hi.at(b, c + 1))
                dve.scalar_tensor_tensor(vx[:, 1, c], rows.bank(f"x{c}")[:, 0:E], X_VX / X_W, vx[:, 0, c],
                                         ALU.mult, ALU.subtract).then_inc(rows.taken.sem, 1)

            def score_max(it, b, c):
                dve.wait_ge(score.ready.sem, score.is_ready(it, f"s{c}"))
                dve.reduce_max(s_nmax[:, c:c + 1], score.bank(f"s{c}")[:, 0:P * (c + 1)], AX.X,
                               negate=True).then_inc(row_max.sem, 1)
                dve.wait_ge(row_max.sem, row_max.at(b, c + 1))
                dve.tensor_scalar(s_bias[:, c:c + 1], s_nmax[:, c:c + 1], 1 / (X_Q * X_H), None,
                                  ALU.mult).then_inc(score_maxed.sem, 1)

            def score_sum(b, c):
                dve.wait_ge(prob_ready.sem, prob_ready.at(b, c + 1))
                dve.tensor_scalar(s_scaled[:, c:c + 1], s_sum[:, c:c + 1], X_P * X_VX, None,
                                  ALU.mult).then_inc(prob_scaled.sem, 1)
                dve.wait_ge(prob_scaled.sem, prob_scaled.at(b, c + 1))
                dve.reciprocal(s_rsum[:, c:c + 1], s_scaled[:, c:c + 1]).then_inc(score.taken.sem, 1)

            def part_prob(b, c):
                dve.wait_ge(probT_hi.sem, probT_hi.at(b, c + 1))
                n = P * (c + 1)
                dve.scalar_tensor_tensor(probT[:, 1, c % 2, 0:n], turned.bank(f"pt{c}")[:, 0:n], X_P,
                                         probT[:, 0, c % 2, 0:n], ALU.mult, ALU.subtract).then_inc(turned.taken.sem, 1)

            def attended(it, c):
                dve.wait_ge(score.taken.sem, score.is_taken(it, f"s{c}"))
                dve.wait_ge(rows.ready.sem, rows.is_ready(it, f"p{c}"))
                dve.scalar_tensor_tensor(x_res[:, c], rows.bank(f"p{c}")[:, 0:E], s_rsum[:, c:c + 1], x_res[:, c],
                                         ALU.mult, ALU.add).then_inc(rows.taken.sem, 1)

            def gate(it, b, j):
                to = gated[:, j % SLOTS]
                dve.wait_ge(tanh_done.sem, tanh_done.at(b, j + 1))
                dve.scalar_tensor_tensor(to, to, 1.0, score.bank(f"g{j}")[:], ALU.add,
                                         ALU.mult).then_inc(score.taken.sem, 1)
                dve.wait_ge(score.taken.sem, score.is_taken(it, f"g{j}"))
                dve.wait_ge(rows.ready.sem, rows.is_ready(it, f"u{j}"))
                scale = X_MID / (2 * (X_H * X_W) ** 2)
                if j < NSH:
                    dve.scalar_tensor_tensor(to, to, scale, rows.bank(f"u{j}")[:], ALU.mult,
                                             ALU.mult).then_inc(rows.taken.sem, 1)
                    dve.wait_ge(rows.taken.sem, rows.is_taken(it, f"u{j}"))
                    dve.sem_inc(gated_done.sem, 1)
                else:
                    dve.scalar_tensor_tensor(to, to, scale / X_COMB, rows.bank(f"u{j}")[:], ALU.mult,
                                             ALU.mult).then_inc(rows.taken.sem, 1)
                    dve.wait_ge(rows.taken.sem, rows.is_taken(it, f"u{j}"))
                    dve.wait_ge(turned.ready.sem, turned.is_ready(it, f"cb{j}"))
                    dve.tensor_tensor(to, to, turned.bank(f"cb{j}")[:], ALU.mult).then_inc(turned.taken.sem, 1)
                    dve.wait_ge(turned.taken.sem, turned.is_taken(it, f"cb{j}"))
                    dve.sem_inc(comb_done.sem, 1)

            def route(it, b):
                dve.wait_ge(rows.ready.sem, rows.is_ready(it, "logit"))
                dve.tensor_scalar(logit[:], rows.bank("logit")[:, 0:C * NE].rearrange("p (c e) -> p c e", c=C),
                                  1 / (X_H * X_W), None, ALU.mult).then_inc(rows.taken.sem, 1)
                hold(dve, rows.taken, rows.is_taken(it, "logit"))
                for c in range(C):
                    last = dve.max(top[:, c], logit[:, c])
                last.then_inc(topped.sem, 1)
                hold(dve, topped, topped.at(b, 1))
                for c in range(C):
                    last = dve.max_index(top_i[:, c], top[:, c], logit[:, c])
                last.then_inc(top_found.sem, 1)
                dve.tensor_tensor(e2_in[:], top[:, :, 1], top[:, :, 0], ALU.subtract).then_inc(shifted.sem, 1)
                dve.tensor_tensor(l_shift[:], logit[:], top[:, :, 0:1].to_broadcast([P, C, NE]),
                                  ALU.subtract).then_inc(shifted.sem, 1)
                dve.wait_ge(top_found.sem, top_found.at(b, 1))
                dve.tensor_copy(top_f[:], top_i[:, :, 0:2]).then_inc(weighed.sem, 1)

            def weigh(b):
                dve.wait_ge(l_exped.sem, l_exped.at(b, 2))
                dve.reduce_sum(l_sum[:], l_exp[:], AX.X).then_inc(weighed.sem, 1)
                dve.tensor_scalar(w_one[:], e2[:], 1.0, None, ALU.add).then_inc(weighed.sem, 1)
                dve.wait_ge(weighed.sem, weighed.at(b, 3))
                dve.scalar_tensor_tensor(w_den[:], l_sum[:], 1e-9, w_one[:], ALU.mult, ALU.add).then_inc(weighed.sem, 1)
                dve.wait_ge(weighed.sem, weighed.at(b, 4))
                dve.tensor_scalar(w_scaled[:], w_den[:], 1 / X_COMB, None, ALU.mult).then_inc(weighed.sem, 1)
                dve.wait_ge(weighed.sem, weighed.at(b, 5))
                dve.reciprocal(w_1[:], w_scaled[:]).then_inc(weighed.sem, 1)
                dve.wait_ge(weighed.sem, weighed.at(b, 6))
                dve.tensor_tensor(w_2[:], w_1[:], e2[:], ALU.mult).then_inc(weighed.sem, 1)
                dve.wait_ge(weighed.sem, weighed.at(b, 7))
                for c in range(C):
                    dve.tensor_scalar(comb1[:, c], expert_no[:], top_f[:, c, 0:1], w_1[:, c:c + 1],
                                      ALU.is_equal, ALU.mult)
                    last = dve.tensor_scalar(comb2[:, c], expert_no[:], top_f[:, c, 1:2], w_2[:, c:c + 1],
                                             ALU.is_equal, ALU.mult)
                last.then_inc(weighed.sem, 1)
                dve.wait_ge(weighed.sem, weighed.at(b, 8))
                dve.tensor_tensor(comb[:], comb1[:], comb2[:], ALU.add).then_inc(weighed.sem, 1)

            def absent(banks, it, *uses):
                banks.skip(dve, banks.taken, it, *uses)

            def iteration(it, f, m, d):
                if f:
                    dve.wait_ge(x_loaded.sem, x_loaded.at(it, 16))
                    statistics(it, 0, x_in)
                if d:
                    part_turned(it - 2, h3T, h3T_hi, "h3")
                else:
                    absent(turned, it, "h3.0", "h3.1")
                if f:
                    normalise(it, it, 0, x_in, h1)
                    part_turned(it, h1T, h1T_hi, "h1", reverse=True)
                    dve.wait_ge(score.ready.sem, score.is_ready(it, "z"))
                    dve.reduce_max(z_nmax[:], score.bank("z")[0:H, :], AX.X, negate=True).then_inc(z_maxed.sem, 1)
                    dve.wait_ge(z_maxed.sem, z_maxed.at(it, 1))
                    dve.tensor_scalar(z_bias[:], z_nmax[:], D ** -0.5 / (X_H * X_W), None,
                                      ALU.mult).then_inc(z_maxed.sem, 1)
                    for c in range(C):
                        if c == 2:
                            dve.wait_ge(z_exped.sem, z_exped.at(it, 1))
                            dve.reciprocal(z_rsum[:], z_sum[:]).then_inc(score.taken.sem, 1)
                        dve.wait_ge(val_hi.sem, val_hi.at(it, c + 1))
                        dve.scalar_tensor_tensor(
                            val[:, 1, :, c], rows.bank(f"v{c}")[:, 0:E].rearrange("p (h d) -> p h d", h=H),
                            X_V / (X_H * X_W), val[:, 0, :, c], ALU.mult, ALU.subtract).then_inc(rows.taken.sem, 1)
                else:
                    absent(turned, it, "h1.0", "h1.1")
                    absent(score, it, "z")
                    absent(rows, it, "v0", "v1", "v2", "v3")
                if m:
                    part_turned(it - 1, mixT, mixT_hi, "mix")
                else:
                    absent(turned, it, "mix.0", "mix.1")
                if d:
                    route(it, it - 2)
                else:
                    absent(rows, it, "logit")
                if m:
                    part_context(it - 1, 0)
                    part_context(it - 1, 1)
                    dve.wait_ge(x_biased.sem, x_biased.at(it - 1, 1))
                    dve.wait_ge(x_kept.sem, x_kept.at(it - 2, 1))
                    for c in range(C):
                        dve.wait_ge(rows.ready.sem, rows.is_ready(it, f"o{c}"))
                        dve.scalar_tensor_tensor(x_res[:, c], rows.bank(f"o{c}")[:, 0:E], 1 / (X_MIX * X_W),
                                                 x_bo[:, c], ALU.mult, ALU.add).then_inc(rows.taken.sem, 1)
                    hold(dve, rows.taken, rows.is_taken(it, "o3"))
                    statistics(it - 1, 1, x_res)
                    part_context(it - 1, 2)
                    part_context(it - 1, 3)
                    for k in range(K2):
                        dve.wait_ge(q_hi.sem, q_hi.at(it - 1, k + 1))
                        dve.scalar_tensor_tensor(qT[:, 1, k], wide[:, k], X_Q / X_QK, qT[:, 0, k], ALU.mult,
                                                 ALU.subtract).then_inc(q_split.sem, 1)
                    normalise(it - 1, it, 1, x_res, h2)
                else:
                    absent(rows, it, "x0", "x1", "o0", "o1", "o2", "o3", "x2", "x3")
                if d:
                    gate(it, it - 2, 0)
                else:
                    absent(score, it, "g0", "g1")
                    absent(rows, it, "u0", "u1", "u2", "u3")
                if m:
                    part_turned(it - 1, h2T, h2T_hi, "h2")
                else:
                    absent(turned, it, "h2.0", "h2.1")
                if d:
                    weigh(it - 2)
                    gate(it, it - 2, 1)
                    dve.wait_ge(turned.ready.sem, turned.is_ready(it, "combT"))
                    dve.tensor_copy(combT[:, 0], turned.bank("combT")[0:NE, :]).then_inc(combT_hi.sem, 1)
                    dve.wait_ge(combT_hi.sem, combT_hi.at(it - 2, 1))
                    dve.tensor_tensor(combT[:, 1], turned.bank("combT")[0:NE, :], combT[:, 0],
                                      ALU.subtract).then_inc(turned.taken.sem, 1)
                else:
                    absent(turned, it, "combT", "cb2")
                if m:
                    score_max(it, it - 1, 0)
                    score_max(it, it - 1, 1)
                    score_sum(it - 1, 0)
                    score_sum(it - 1, 1)
                else:
                    absent(score, it, "s0", "s1")
                for c in range(C):
                    if d:
                        gate(it, it - 2, c + 2)
                    elif c:
                        absent(turned, it, f"cb{c + 2}")
                    if not d:
                        absent(score, it, f"g{c + 2}")
                        if c >= 2:
                            absent(rows, it, f"u{c + 2}")
                    if m:
                        if c:
                            attended(it, c - 1)
                        part_prob(it - 1, c)
                        if c < 2:
                            score_max(it, it - 1, c + 2)
                            score_sum(it - 1, c + 2)
                    else:
                        if c:
                            absent(rows, it, f"p{c - 1}")
                        absent(turned, it, f"pt{c}")
                        if c < 2:
                            absent(score, it, f"s{c + 2}")
                if d:
                    gate(it, it - 2, 6)
                else:
                    absent(score, it, "g6", "g7", "g8", "g9", "none")
                    absent(turned, it, "cb6", "cb7", "cb8", "cb9", "none")
                    absent(rows, it, "u6")
                if m:
                    attended(it, 3)
                    hold(dve, rows.taken, rows.is_taken(it, "p3"))
                    statistics(it - 1, 2, x_res)
                else:
                    absent(rows, it, "p3")
                if d:
                    gate(it, it - 2, 7)
                else:
                    absent(rows, it, "u7", "u8", "u9", "none")
                if m:
                    normalise(it - 1, it, 2, x_res, h3)
                if d:
                    gate(it, it - 2, 8)
                    gate(it, it - 2, 9)
                    for banks in (turned, score, rows):
                        absent(banks, it, "none")
                    dve.wait_ge(x_kept.sem, x_kept.at(it - 2, 1))
                    dve.wait_ge(y_ready.sem, y_ready.at(it - 2, 1))
                    for g in range(2):
                        last = dve.scalar_tensor_tensor(
                            x_out[:, 2 * g:2 * g + 2], wide[:, g].rearrange("p (c e) -> p c e", c=2),
                            1 / (X_MID * X_W), x_out[:, 2 * g:2 * g + 2], ALU.mult, ALU.add)
                    last.then_inc(y_taken.sem, 1)

            early, late = range(EARLY), range(EARLY, len(loads))
            part_weights(early)
            iteration(0, True, False, False)
            part_product()
            part_weights(late)
            iteration(1, True, True, False)
            with dve.Fori(2, B) as it:
                iteration(it, True, True, True)
            iteration(B, False, True, True)
            iteration(B + 1, False, False, True)

        @block.tensor
        def _(pe):
            for banks in (turned, score, rows):
                pe.sem_inc(banks.ready.sem, len(banks.order))
            pe.sem_inc(q_ready.sem, 2)
            pe.wait_ge(const_made, 11)

            def turn(it, use, src):
                for k in range(K2):
                    pe.wait_ge(turned.taken.sem, turned.is_free(it, f"{use}.{k}"))
                    for c in range(C):
                        last = pe.transpose(turned.bank(f"{use}.{k}")[:, P * c:P * c + P], src[:, c, P * k:P * k + P],
                                            ident[:])
                    last.then_inc(turned.ready.sem, 1)

            def project(it, use, src, w, c):
                pe.wait_ge(rows.taken.sem, rows.is_free(it, use))
                for k in range(K2):
                    last = three_passes(pe, rows.bank(use)[:, 0:E], parts(src, k, slice(P * c, P * c + P)),
                                        parts(w, k, slice(None)), start=(k == 0), stop=(k == K2 - 1))
                last.then_inc(rows.ready.sem, 1)

            def toeplitz(it, b, g):
                if g == 0:
                    pe.wait_ge(toep_loaded.sem, toep_loaded.at(b, 32))
                    pe.wait_ge(rows.taken.sem, rows.is_taken(it - 1, "v3"))
                    pe.wait_ge(y_taken.sem, y_taken.at(b, -1))
                for n in range(H // 2):
                    head = H // 2 * g + n
                    acc = wide[:, g, C * D * n:C * D * (n + 1)].rearrange("p (c d) -> p c d", c=C)
                    for delta in range(C):
                        last = three_passes(pe, acc[:, delta:C, :], parts(toep, head, slice(P * delta, P * delta + P)),
                                            parts(val, head, slice(0, C - delta), slice(None)),
                                            start=(delta == 0), stop=(delta == C - 1), skip_group_check=True)
                last.then_inc(mix_ready.sem, 1)

            def scores(it, c):
                n = P * (c + 1)
                to = score.bank(f"s{c}")
                pe.wait_ge(score.taken.sem, score.is_free(it, f"s{c}"))
                for k in range(K2):
                    three_passes(pe, to[:, 0:n], parts(qT, k, slice(P * c, P * c + P)), parts(h2T, k, slice(0, n)),
                                 start=(k == 0), stop=False, skip_group_check=True)
                pe.matmul(to[:, n - P:n], ident16[:], future[:], start=False, stop=True,
                          skip_group_check=True).then_inc(score.ready.sem, 1)

            def turn_probs(it, b, c):
                pe.wait_ge(turned.taken.sem, turned.is_free(it, f"pt{c}"))
                pe.wait_ge(prob_ready.sem, prob_ready.at(b, c + 1))
                for t in range(c + 1):
                    last = pe.transpose(turned.bank(f"pt{c}")[:, P * t:P * t + P], prob[:, c % 2, P * t:P * t + P],
                                        ident[:])
                last.then_inc(turned.ready.sem, 1)

            def attend(it, c):
                pe.wait_ge(rows.taken.sem, rows.is_free(it, f"p{c}"))
                pe.wait_ge(turned.taken.sem, turned.is_taken(it, f"pt{c}"))
                for t in range(c + 1):
                    last = three_passes(pe, rows.bank(f"p{c}")[:, 0:E], parts(probT, c % 2, slice(P * t, P * t + P)),
                                        parts(vx, t, slice(None)), start=(t == 0), stop=(t == c))
                last.then_inc(rows.ready.sem, 1)

            def gate_up(it, j):
                for at, banks, use in ((0, score, f"g{j}"), (P, rows, f"u{j}")):
                    pe.wait_ge(banks.taken.sem, banks.is_free(it, use))
                    for k in range(K2):
                        last = three_passes(pe, banks.bank(use)[:],
                                            parts(w_gu, k, slice(2 * P * j + at, 2 * P * j + at + P)),
                                            parts(h3T, k, slice(None)), start=(k == 0), stop=(k == K2 - 1))
                    last.then_inc(banks.ready.sem, 1)
                if j >= NSH:
                    pe.wait_ge(turned.taken.sem, turned.is_free(it, f"cb{j}"))
                    pe.wait_ge(turned.taken.sem, turned.is_taken(it, "combT"))
                    for a in range(2):
                        last = pe.matmul(turned.bank(f"cb{j}")[:], spread[:, j - NSH, :], combT[:, a, :],
                                         start=(a == 0), stop=(a == 1))
                    last.then_inc(turned.ready.sem, 1)

            def down(b, j):
                pe.wait_ge(mid_split.sem, mid_split.at(b, j + 1))
                for c in range(C):
                    last = three_passes(pe, wide[:, c // 2, E * (c % 2):E * (c % 2) + E],
                                        parts(mid, j % SLOTS, slice(P * c, P * c + P)), parts(w_d, j, slice(None)),
                                        start=(j == 0 and c % 2 == 0), stop=(j == MID - 1), skip_group_check=True)
                if j == MID - 1:
                    last.then_inc(y_ready.sem, 1)

            def absent(banks, it, *uses):
                banks.skip(pe, banks.ready, it, *uses)

            def iteration(it, f, m, d):
                if m:
                    toeplitz(it, it - 1, 0)
                if d:
                    pe.wait_ge(h_ready[2].sem, h_ready[2].at(it - 2, 1))
                    turn(it, "h3", h3)
                else:
                    absent(turned, it, "h3.0", "h3.1")
                if f:
                    pe.wait_ge(h_ready[0].sem, h_ready[0].at(it, 1))
                    turn(it, "h1", h1)
                else:
                    absent(turned, it, "h1.0", "h1.1")
                if m:
                    toeplitz(it, it - 1, 1)
                if f:
                    pe.wait_ge(turned.taken.sem, turned.is_taken(it, "h1.1"))
                    pe.wait_ge(score.taken.sem, score.is_free(it, "z"))
                    for k in range(K2):
                        last = three_passes(pe, score.bank("z")[0:H, :], parts(w_a, k, slice(None)),
                                            parts(h1T, k, slice(None)), start=(k == 0), stop=(k == K2 - 1))
                    last.then_inc(score.ready.sem, 1)
                    for c in range(C):
                        project(it, f"v{c}", h1T, w_v, c)
                else:
                    absent(score, it, "z")
                    absent(rows, it, "v0", "v1", "v2", "v3")
                if m:
                    pe.wait_ge(mix_taken.sem, mix_taken.at(it - 1, 2))
                    turn(it, "mix", mix)
                else:
                    absent(turned, it, "mix.0", "mix.1")
                if d:
                    pe.wait_ge(rows.taken.sem, rows.is_free(it, "logit"))
                    pe.wait_ge(turned.taken.sem, turned.is_taken(it, "h3.1"))
                    for c in range(C):
                        for k in range(K2):
                            last = three_passes(pe, rows.bank("logit")[:, NE * c:NE * c + NE],
                                                parts(h3T, k, slice(P * c, P * c + P)), parts(w_r, k, slice(None)),
                                                start=(k == 0), stop=(k == K2 - 1))
                    last.then_inc(rows.ready.sem, 1)
                else:
                    absent(rows, it, "logit")
                if m:
                    pe.wait_ge(c_split.sem, c_split.at(it - 1, 1))
                    project(it, "x0", cT, w_vx, 0)
                    project(it, "x1", cT, w_vx, 1)
                    pe.wait_ge(turned.taken.sem, turned.is_taken(it, "mix.1"))
                    for c in range(C):
                        project(it, f"o{c}", mixT, w_o, c)
                    project(it, "x2", cT, w_vx, 2)
                    project(it, "x3", cT, w_vx, 3)
                    for n in range(K2):
                        for k in range(K2):
                            last = three_passes(pe, wide[:, n], parts(w_qk, k, slice(P * n, P * n + P)),
                                                parts(cT, k, slice(None)), start=(k == 0), stop=(k == K2 - 1))
                        last.then_inc(q_ready.sem, 1)
                else:
                    absent(rows, it, "x0", "x1", "o0", "o1", "o2", "o3", "x2", "x3")
                if d:
                    gate_up(it, 0)
                else:
                    absent(score, it, "g0", "g1")
                    absent(rows, it, "u0", "u1", "u2", "u3")
                if m:
                    pe.wait_ge(h_ready[1].sem, h_ready[1].at(it - 1, 1))
                    turn(it, "h2", h2)
                else:
                    absent(turned, it, "h2.0", "h2.1")
                if d:
                    gate_up(it, 1)
                    pe.wait_ge(turned.taken.sem, turned.is_free(it, "combT"))
                    pe.wait_ge(weighed.sem, weighed.at(it - 2, 9))
                    for c in range(C):
                        last = pe.transpose(turned.bank("combT")[0:NE, P * c:P * c + P], comb[:, c], ident[:])
                    last.then_inc(turned.ready.sem, 1)
                    if m:
                        pe.wait_ge(q_split.sem, q_split.at(it - 1, 2))
                    else:
                        pe.wait_ge(y_taken.sem, y_taken.at(it - 2, 0))
                else:
                    absent(turned, it, "combT", "cb2")
                if m:
                    pe.wait_ge(turned.taken.sem, turned.is_taken(it, "h2.1"))
                    pe.wait_ge(q_split.sem, q_split.at(it - 1, 2))
                    scores(it, 0)
                    scores(it, 1)
                else:
                    absent(score, it, "s0", "s1")
                for c in range(C):
                    if d:
                        gate_up(it, c + 2)
                        down(it - 2, c)
                    elif c:
                        absent(turned, it, f"cb{c + 2}")
                    if not d:
                        absent(score, it, f"g{c + 2}")
                        if c >= 2:
                            absent(rows, it, f"u{c + 2}")
                    if m:
                        if c:
                            attend(it, c - 1)
                        turn_probs(it, it - 1, c)
                        if c < 2:
                            scores(it, c + 2)
                    else:
                        if c:
                            absent(rows, it, f"p{c - 1}")
                        absent(turned, it, f"pt{c}")
                        if c < 2:
                            absent(score, it, f"s{c + 2}")
                if d:
                    gate_up(it, 6)
                    down(it - 2, 4)
                else:
                    absent(score, it, "g6", "g7", "g8", "g9", "none")
                    absent(turned, it, "cb6", "cb7", "cb8", "cb9", "none")
                    absent(rows, it, "u6")
                if m:
                    attend(it, 3)
                else:
                    absent(rows, it, "p3")
                if d:
                    for j in range(7, MID):
                        gate_up(it, j)
                        down(it - 2, j - 2)
                    down(it - 2, MID - 2)
                    down(it - 2, MID - 1)
                    for banks in (turned, score, rows):
                        absent(banks, it, "none")
                else:
                    absent(rows, it, "u7", "u8", "u9", "none")

            pe.wait_ge(w_lo, EARLY)
            iteration(0, True, False, False)
            for n in range(K2):
                for k in range(K2):
                    last = three_passes(pe, wide[:, n, 0:E], parts(w_q, k, slice(P * n, P * n + P)),
                                        parts(w_k, k, slice(None)), start=(k == 0), stop=(k == K2 - 1))
                last.then_inc(qk_product, 1)
            pe.wait_ge(qk_lo, 2)
            pe.wait_ge(w_lo, len(loads))
            iteration(1, True, True, False)
            with pe.Fori(2, B) as it:
                iteration(it, True, True, True)
            iteration(B, False, True, True)
            iteration(B + 1, False, False, True)


def kernel(x, ctx_1024, L0_attn_W_A, L0_attn_W_V, L0_attn_W_O, L0_attn_b_O, L0_xattn_WK, L0_xattn_WV,
           L0_xattn_WQ, L0_ffn_router_w, L0_ffn_wg_r, L0_ffn_wu_r, L0_ffn_wd_r, L0_ffn_wg_s, L0_ffn_wu_s,
           L0_ffn_wd_s):
    import numpy as np
    import concourse.bacc as bacc
    from concourse.bass_utils import run_bass_kernel_spmd

    def gate_up_columns(g, u):
        n, d, m = g.shape
        g, u = (np.transpose(np.asarray(w), (1, 0, 2)).reshape(d, n * m // P, 1, P) for w in (g, u))
        return np.ascontiguousarray(np.concatenate([g, u], axis=2).reshape(d, 2 * n * m))

    arrays = {
        "x": np.asarray(x),
        "ctxT": np.ascontiguousarray(np.transpose(np.asarray(ctx_1024), (0, 2, 1))),
        "wa": np.ascontiguousarray(np.asarray(L0_attn_W_A).T),
        "wv": np.ascontiguousarray(np.asarray(L0_attn_W_V).T),
        "wo": np.ascontiguousarray(np.asarray(L0_attn_W_O).T),
        "bo": np.asarray(L0_attn_b_O),
        "wq": np.ascontiguousarray(np.asarray(L0_xattn_WQ).T),
        "wk": np.ascontiguousarray(np.asarray(L0_xattn_WK).T),
        "wvx": np.asarray(L0_xattn_WV),
        "rw": np.asarray(L0_ffn_router_w),
        "gu_s": gate_up_columns(L0_ffn_wg_s, L0_ffn_wu_s),
        "wd_s": np.asarray(L0_ffn_wd_s).reshape(-1, E),
        "gu_r": gate_up_columns(L0_ffn_wg_r, L0_ffn_wu_r),
        "wd_r": np.asarray(L0_ffn_wd_r).reshape(-1, E),
    }
    nc = bacc.Bacc("TRN2", target_bir_lowering=False, num_devices=1)
    args = [nc.dram_tensor(f"in_{n}", a.shape, mybir.dt.from_np(a.dtype), kind="ExternalInput").ap()
            for n, a in arrays.items()]
    out = nc.dram_tensor("out_0", (B, S, E), F32, kind="ExternalOutput").ap()
    decoder_layer(nc, *args, out)
    r = run_bass_kernel_spmd(nc, [{f"in_{n}": a for n, a in arrays.items()}], core_ids=[0])
    return r.results[0]["out_0"]
```

```python
from contextlib import ExitStack

import concourse.bass as bass
from concourse import mybir

P = 128
ALU = mybir.AluOpType
ACT = mybir.ActivationFunctionType
AX = mybir.AxisListType
F32 = mybir.dt.float32
F16 = mybir.dt.float16
BF16 = mybir.dt.bfloat16
U32 = mybir.dt.uint32
I32 = mybir.dt.int32

B, S, E = 8, 512, 256
H, D = 16, 16
NE, MR = 16, 64
C = S // P
K2 = E // P
NSH = 2
PAIRS = NE * MR // P
MID = NSH + PAIRS
PAD = P
ZROW = PAD + S
EPS = 1e-5
NEG = -1e30
SLOTS = 3

X_H = 256.0
X_W = 64.0
X_Z = 4096.0
X_V = 16.0
X_MIX = 64.0
X_QK = 1024.0
X_Q = 256.0
X_VX = 16.0
X_P = 4096.0
X_MID = 16.0

TURNED = ["mix.0", "mix.1", "combT", "h2.0", "h2.1", "pt0", "pt1", "pt2", "pt3", "h3.0", "h3.1", "h1.0", "h1.1", "none"]
SCORE = ["z", "g0", "g1", "s0", "s1", "g2", "s2", "g3", "s3", "g4", "g5", "g6", "g7", "g8", "g9", "none"]
ROWS = (["logit", "v0", "v2", "x0", "o0", "o2", "x2", "u0", "u1", "u2", "u3", "p0", "u4", "p1", "u5", "p2"]
        + ["u6", "p3", "u7", "u8", "u9", "none"])


class Signal:

    def __init__(self, sem, per_round, before=0):
        self.sem, self.per_round, self.before = sem, per_round, before

    def at(self, n, count):
        return n * self.per_round + (count + self.before)


class Banks:

    def __init__(self, order, banks, ready, taken):
        assert len(order) % 2 == 0
        self.order, self.banks = order, banks
        self.reached = {}
        n = len(order)
        self.ready, self.taken = Signal(ready, n, n), Signal(taken, n, n)

    def bank(self, use):
        return self.banks[self.order.index(use) % 2]

    def is_ready(self, it, use):
        return self.ready.at(it, self.order.index(use) + 1)

    def was_ready(self, it, use):
        return self.ready.at(it, self.order.index(use) + 1 - len(self.order))

    def is_taken(self, it, use):
        return self.taken.at(it, self.order.index(use) + 1)

    def is_free(self, it, use):
        return self.taken.at(it, self.order.index(use) - 1)

    def reach(self, eng, signal, it, use=None):
        key = (id(eng), signal is self.ready)
        at = self.reached.get(key, 0)
        to = len(self.order) if use is None else self.order.index(use)
        if to > at:
            eng.wait_ge(signal.sem, signal.at(it, at))
            eng.sem_inc(signal.sem, to - at)
        self.reached[key] = 0 if use is None else to + 1

    def fill(self, pe, it, use):
        self.reach(pe, self.ready, it, use)
        pe.wait_ge(self.taken.sem, self.is_free(it, use))

    def take(self, dve, it, use):
        self.reach(dve, self.taken, it, use)

    def begin(self, eng, signal, use):
        eng.sem_inc(signal.sem, self.order.index(use))
        self.reached[(id(eng), signal is self.ready)] = self.order.index(use)


def three_passes(pe, out, stationary, moving, start, stop, **kw):
    pe.matmul(out, stationary[0], moving[0], start=start, stop=False, **kw)
    pe.matmul(out, stationary[0], moving[1], start=False, stop=False, **kw)
    return pe.matmul(out, stationary[1], moving[0], start=False, stop=stop, **kw)


def decoder_layer(nc, x, ctxT, wa, wv, wo, bo, wq, wk, wvx, rw, gu_s, wd_s, gu_r, wd_r, out):
    with ExitStack() as ctx:
        def sb(name, shape, dt=F32):
            return ctx.enter_context(nc.sbuf_tensor(name, shape, dt))

        def bank(name, shape=(P, 512), dt=F32):
            return ctx.enter_context(nc.psum_tensor(name, list(shape), dt))

        def sem(name):
            return ctx.enter_context(nc.semaphore(name))

        def sig(name, per_batch, before=0):
            return Signal(sem(name), per_batch, before)

        w_a = sb("w_a", [P, 2, K2, H], F16)
        w_v = sb("w_v", [P, 2, K2, E], F16)
        w_o = sb("w_o", [P, 2, K2, E], F16)
        w_q = sb("w_q", [P, 2, K2, E], F16)
        w_k = sb("w_k", [P, 2, K2, E], F16)
        w_qk = sb("w_qk", [P, 2, K2, E], F16)
        w_vx = sb("w_vx", [P, 2, K2, E], F16)
        w_r = sb("w_r", [P, 2, K2, NE], F16)
        w_gu = sb("w_gu", [P, 2, K2, 2 * MID * P], F16)
        w_d = sb("w_d", [P, 2, MID, E], F16)
        NS, NR = 2 * NSH * P, 2 * PAIRS * P

        ident = sb("ident", [P, P])
        ident16 = sb("ident16", [P, P], BF16)
        future = sb("future", [P, P], BF16)
        expert_no_i = sb("expert_no_i", [P, NE], I32)
        expert_no = sb("expert_no", [P, NE])
        zeros16 = sb("zeros16", [P, B * 2 * H // P, PAD], F16)
        minus_half = sb("minus_half", [P, C])
        b_o = sb("b_o", [P, E])

        x_in = sb("x_in", [P, C, E])
        x_bo = sb("x_bo", [P, C, E])
        h1 = sb("h1", [P, C, E])
        h1T = sb("h1T", [P, 2, K2, S], F16)
        z_nmax = sb("z_nmax", [H, 1])
        z_bias = sb("z_bias", [H, 1])
        z_exp = sb("z_exp", [H, S])
        z_sum = sb("z_sum", [H, 1])
        z_rsum = sb("z_rsum", [H, 1])
        z_norm = sb("z_norm", [H, S])
        z_parts = sb("z_parts", [H, 2, S], F16)
        toep = sb("toep", [P, 2, H, S], F16)
        val = sb("val", [P, 2, C, E], F16)
        cT_in = sb("cT_in", [P, K2, S])
        cT = sb("cT", [P, 2, K2, S], F16)

        mix = sb("mix", [P, C, E])
        mixT = sb("mixT", [P, 2, K2, S], F16)
        vx = sb("vx", [P, 2, C, E], F16)
        qT = sb("qT", [P, 2, K2, S], F16)
        x_res = sb("x_res", [P, C, E])
        h2 = sb("h2", [P, C, E])
        h2T = sb("h2T", [P, 2, K2, S], F16)
        s_nmax = sb("s_nmax", [P, C])
        s_bias = sb("s_bias", [P, C])
        s_sum = sb("s_sum", [P, C])
        s_scaled = sb("s_scaled", [P, C])
        s_rsum = sb("s_rsum", [P, C])
        prob = sb("prob", [P, 2, S])
        probT = sb("probT", [P, 2, 2, S], F16)
        h3 = sb("h3", [P, C, E])

        x_out = sb("x_out", [P, C, E])
        h3T = sb("h3T", [P, 2, K2, S], F16)
        logit = sb("logit", [P, C, NE])
        top = sb("top", [P, C, 8])
        top_i = sb("top_i", [P, C, 8], U32)
        top_f = sb("top_f", [P, C, 2])
        l_shift = sb("l_shift", [P, C, NE])
        l_exp = sb("l_exp", [P, C, NE])
        e2_in = sb("e2_in", [P, C])
        e2 = sb("e2", [P, C])
        l_sum = sb("l_sum", [P, C])
        w_one = sb("w_one", [P, C])
        w_den = sb("w_den", [P, C])
        w_1 = sb("w_1", [P, C])
        w_2 = sb("w_2", [P, C])
        comb1 = sb("comb1", [P, C, NE])
        comb2 = sb("comb2", [P, C, NE])
        comb = sb("comb", [P, C, NE])
        combT = sb("combT", [NE, S])
        gated = sb("gated", [P, SLOTS, S])
        mid = sb("mid", [P, 2, SLOTS, S], F16)

        stats = [sb(f"stats{n}", [P, C, 6]) for n in range(3)]
        mean_var = [sb(f"mean_var{n}", [P, C, 2]) for n in range(3)]
        var_eps = [sb(f"var_eps{n}", [P, C]) for n in range(3)]
        rstd = [sb(f"rstd{n}", [P, C]) for n in range(3)]

        loads = [
            ("wa", wa, w_a, K2, H),
            ("wv", wv, w_v, K2, E),
            ("wq", wq, w_q, K2, E),
            ("wk", wk, w_k, K2, E),
            ("wvx", wvx, w_vx, K2, E),
            ("wo", wo, w_o, K2, E),
            ("rw", rw, w_r, K2, NE),
            ("gu_s", gu_s, w_gu[:, :, :, 0:NS], K2, NS),
            ("wd_s", wd_s, w_d[:, :, 0:NSH], NSH, E),
            ("gu_r", gu_r, w_gu[:, :, :, NS:NS + NR], K2, NR),
            ("wd_r", wd_r, w_d[:, :, NSH:MID], PAIRS, E),
        ]
        names = [n for n, *_ in loads]
        EARLY, MIDDLE = names.index("wk") + 1, names.index("rw")
        borrowed = {"gu_s": (x_out, 0), "wd_s": (h3, 0), "wo": (h3, 2), "wvx": (x_res, 0)}
        stage = sb("stage", [P, sum(k * n for name, _, _, k, n in loads if name not in borrowed)])
        staged, at = {}, 0
        for name, _, _, k, n in loads:
            if name in borrowed:
                buffer, c = borrowed[name]
                flat = buffer[:, c:c + k * n // E].rearrange("p c e -> p (c e)")
            else:
                flat = stage[:, at:at + k * n]
                at += k * n
            staged[name] = flat.rearrange("p (k n) -> p k n", k=k)
        comb_rows = stage[:, 0:PAIRS * S].rearrange("p (q s) -> p q s", q=PAIRS)

        turned = Banks(TURNED, [bank(f"turned{k}") for k in range(2)], sem("turned_ready"), sem("turned_taken"))
        score = Banks(SCORE, [bank(f"score{k}") for k in range(2)], sem("score_ready"), sem("score_taken"))
        rows = Banks(ROWS, [bank(f"rows{k}") for k in range(2)], sem("rows_ready"), sem("rows_taken"))
        wide = bank("wide", [P, 2, 512])

        comb_dram = nc.dram_tensor("comb_scratch", [NE, S], F32, kind="Internal").ap()
        z_dram = nc.dram_tensor("z_scratch", [B, 2 * H, ZROW], F16, kind="Internal").ap()

        w_loaded = [sem(f"loaded_{n}") for n, *_ in loads]
        w_hi = sem("w_hi")
        w_lo = sem("w_lo")
        qk_product = sem("qk_product")
        qk_hi = sem("qk_hi")
        qk_lo = sem("qk_lo")
        const_made = sem("const_made")
        pads_stored = sem("pads_stored")
        bo_loaded = sem("bo_loaded")
        held = {eng.engine: sem(f"held_{n}") for n, eng in (("dve", nc.vector), ("pool", nc.gpsimd))}

        x_loaded = sig("x_loaded", 16)
        c_loaded = sig("c_loaded", 16)
        z_stored = sig("z_stored", 16)
        toep_loaded = sig("toep_loaded", 32)
        y_stored = sig("y_stored", 16, 16)
        stats_done = [sig(f"stats_done{n}", 1) for n in range(3)]
        aggr_done = [sig(f"aggr_done{n}", 1) for n in range(3)]
        eps_added = [sig(f"eps_added{n}", 1) for n in range(3)]
        rstd_done = [sig(f"rstd_done{n}", 1) for n in range(3)]
        h_ready = [sig(f"h_ready{n}", 1, 1) for n in range(3)]
        x_biased = sig("x_biased", 1, 1)
        c_hi = sig("c_hi", K2)
        c_split = sig("c_split", K2, K2)
        h1T_hi = sig("h1T_hi", 2)
        h2T_hi = sig("h2T_hi", 2)
        h3T_hi = sig("h3T_hi", 2)
        mixT_hi = sig("mixT_hi", 2)
        z_maxed = sig("z_maxed", 2)
        z_exped = sig("z_exped", 1)
        z_scaled = sig("z_scaled", 2)
        z_split = sig("z_split", 1)
        val_hi = sig("val_hi", C // 2)
        vx_hi = sig("vx_hi", C // 2)
        mix_ready = sig("mix_ready", 2)
        mix_taken = sig("mix_taken", 2, 2)
        q_ready = sig("q_ready", 2, 2)
        q_hi = sig("q_hi", 2)
        q_split = sig("q_split", 2, 2)
        row_max = sig("row_max", C)
        score_maxed = sig("score_maxed", C)
        prob_ready = sig("prob_ready", C)
        prob_scaled = sig("prob_scaled", C)
        probT_hi = sig("probT_hi", C)
        x_kept = sig("x_kept", 1, 1)
        logit_copied = sig("logit_copied", 1)
        topped = sig("topped", 1)
        top_found = sig("top_found", 1)
        shifted = sig("shifted", 2)
        l_exped = sig("l_exped", 2)
        weighed = sig("weighed", 8)
        comb_stored = sig("comb_stored", 16)
        comb_loaded = [sig(f"comb_loaded{n}", 32) for n in range(2)]
        tanh_done = sig("tanh_done", MID)
        opened = sig("opened", PAIRS)
        gated_done = sig("gated_done", MID)
        mid_hi = sig("mid_hi", MID)
        mid_split = sig("mid_split", MID, MID)
        y_ready = sig("y_ready", 1)
        y_taken = sig("y_taken", 1, 2)

        def hold(eng, signal, value):
            eng.wait_ge(signal.sem, value)
            eng.sem_inc(held[eng.engine], 1)

        def backwards(row):
            return row.rearrange("p (c t) -> p c t", t=P)[:, :, ::-1]

        def parts(t, *index):
            return [t[(slice(None), a, *index)] for a in range(2)]

        def iterations(eng, iteration, start=1):
            if start <= 0:
                iteration(0, True, False, False, True)
            if start <= 1:
                iteration(1, True, True, False, True)
            with eng.Fori(2, B - 1) as it:
                iteration(it, True, True, True, True)
            iteration(B - 1, True, True, True, False)
            iteration(B, False, True, True, False)
            iteration(B + 1, False, False, True, False)

        block = ctx.enter_context(nc.Block())

        @block.sync
        def _(sp):
            def load_x(b):
                sp.wait_ge(h_ready[0].sem, h_ready[0].at(b, 0))
                sp.wait_ge(x_biased.sem, x_biased.at(b, 0))
                sp.dma_start(x_in[:], x[b].rearrange("(c p) e -> p c e", p=P)).then_inc(x_loaded.sem, 16)

            def load_context(b):
                sp.wait_ge(c_split.sem, c_split.at(b, 0))
                sp.dma_start(cT_in[:], ctxT[b].rearrange("(k p) s -> p k s", p=P)).then_inc(c_loaded.sem, 16)

            load_x(0)
            for n, (name, src, _, _, _) in enumerate(loads):
                if n == MIDDLE:
                    sp.wait_ge(const_made, 1)
                    sp.dma_start(z_dram.rearrange("b r s -> (b r) s")[:, 0:PAD].rearrange("(n p) s -> p n s", p=P),
                                 zeros16[:]).then_inc(pads_stored, 16)
                    load_x(1)
                sp.dma_start(staged[name], src.rearrange("(k p) n -> p k n", p=P)).then_inc(w_loaded[n], 16)
                if name == "wk":
                    sp.dma_start(b_o[:], bo.partition_broadcast(P)).then_inc(bo_loaded, 16)
                    load_context(0)
            def iteration(it, f, m, d, n):
                if f:
                    sp.wait_ge(z_split.sem, z_split.at(it, 1))
                    sp.dma_start(z_dram[it, :, PAD:ZROW].rearrange("(a h) s -> h a s", a=2),
                                 z_parts[:]).then_inc(z_stored.sem, 16)
                if d:
                    sp.wait_ge(turned.taken.sem, turned.is_taken(it, "combT"))
                    sp.dma_start(comb_dram, combT[:]).then_inc(comb_stored.sem, 16)
                    sp.wait_ge(comb_stored.sem, comb_stored.at(it - 2, 16))
                    for at in range(0, PAIRS, PAIRS // 2):
                        for g in range(2):
                            rows_of = bass.AP(comb_dram.tensor, comb_dram.offset + (2 * at + g) * S,
                                              [[0, MR], [2 * S, PAIRS // 2], [1, S]])
                            sp.dma_start(comb_rows[MR * g:MR * g + MR, at:at + PAIRS // 2], rows_of)\
                                .then_inc(comb_loaded[2 * at // PAIRS].sem, 16)
                if f:
                    sp.wait_ge(z_stored.sem, z_stored.at(it, 16))
                    if not m:
                        sp.wait_ge(pads_stored, 16)
                    if m:
                        sp.wait_ge(mix_ready.sem, mix_ready.at(it - 1, 2))
                    for a in range(2):
                        src = z_dram[it, a * H:(a + 1) * H, PAD - P + 1:ZROW]
                        skewed = bass.AP(src.tensor, src.offset, [[1, P], [ZROW, H], [1, S]])
                        sp.dma_start(toep[:, a], skewed).then_inc(toep_loaded.sem, 16)
                if n:
                    if m:
                        load_x(it + 1)
                    load_context(it + 1)
                if d:
                    sp.wait_ge(y_taken.sem, y_taken.at(it - 2, 1))
                    sp.dma_start(out[it - 2].rearrange("(c p) e -> p c e", p=P), x_out[:]).then_inc(y_stored.sem, 16)

            iteration(0, True, False, False, True)
            iteration(1, True, True, False, True)
            sp.wait_ge(w_lo, len(loads))
            iterations(sp, iteration, 2)
            sp.wait_ge(y_stored.sem, y_stored.at(B, 0))

        @block.gpsimd
        def _(pool):
            pool.memset(zeros16[:], 0.0).then_inc(const_made, 1)
            pool.memset(ident[:], 0.0).then_inc(const_made, 1)
            pool.memset(future[:], 0.0).then_inc(const_made, 1)
            pool.memset(minus_half[:], -0.5).then_inc(const_made, 1)
            pool.iota(expert_no_i[:], pattern=[[1, NE]], base=0, channel_multiplier=0).then_inc(const_made, 1)
            pool.wait_ge(const_made, 5)
            pool.affine_select(out=ident[:], in_=ident[:], compare_op=ALU.not_equal, fill=1.0, base=0,
                               pattern=[[-1, P]], channel_multiplier=1).then_inc(const_made, 1)
            pool.affine_select(out=future[:], in_=future[:], compare_op=ALU.is_ge, fill=NEG, base=0,
                               pattern=[[-1, P]], channel_multiplier=1).then_inc(const_made, 1)
            pool.tensor_copy(expert_no[:], expert_no_i[:]).then_inc(const_made, 1)
            pool.wait_ge(const_made, 8)
            pool.tensor_copy(ident16[:], ident[:]).then_inc(const_made, 1)
            pool.sem_inc(x_biased.sem, 1)
            pool.sem_inc(c_split.sem, K2)
            pool.sem_inc(x_kept.sem, 1)
            pool.sem_inc(mid_split.sem, MID)

            def reciprocal_deviation(b, n):
                hold(pool, aggr_done[n], aggr_done[n].at(b, 1))
                pool.tensor_scalar(var_eps[n][:], mean_var[n][:, :, 1], EPS, X_H ** -2, ALU.add,
                                   ALU.mult).then_inc(eps_added[n].sem, 1)
                pool.wait_ge(eps_added[n].sem, eps_added[n].at(b, 1))
                pool.tensor_tensor(rstd[n][:], var_eps[n][:], minus_half[:], ALU.pow).then_inc(rstd_done[n].sem, 1)

            def part_mid(b, j):
                pool.wait_ge(mid_hi.sem, mid_hi.at(b, j + 1))
                pool.tensor_tensor(mid[:, 1, j % SLOTS], gated[:, j % SLOTS], mid[:, 0, j % SLOTS],
                                   ALU.subtract).then_inc(mid_split.sem, 1)

            def add_bias(b):
                pool.wait_ge(bo_loaded, 16)
                for c in range(C):
                    last = pool.tensor_tensor(x_bo[:, c], x_in[:, c], b_o[:], ALU.add)
                last.then_inc(x_biased.sem, 1)

            def part_context_columns(b, k):
                pool.wait_ge(c_hi.sem, c_hi.at(b, k + 1))
                pool.tensor_tensor(cT[:, 1, k], cT_in[:, k], cT[:, 0, k], ALU.subtract).then_inc(c_split.sem, 1)

            def iteration(it, f, m, d, n):
                if f and not m:
                    add_bias(it)
                if f:
                    if m:
                        pool.wait_ge(z_stored.sem, z_stored.at(it, 0))
                    hold(pool, score.taken, score.is_taken(it, "z"))
                    pool.tensor_scalar(z_norm[:], z_exp[:], z_rsum[:], X_Z, ALU.mult, ALU.mult)\
                        .then_inc(z_scaled.sem, 1)
                    hold(pool, z_scaled, z_scaled.at(it, 1))
                    pool.tensor_copy(z_parts[:, 0], z_norm[:]).then_inc(z_scaled.sem, 1)
                    pool.wait_ge(z_scaled.sem, z_scaled.at(it, 2))
                    pool.tensor_tensor(z_parts[:, 1], z_norm[:], z_parts[:, 0], ALU.subtract).then_inc(z_split.sem, 1)
                if d:
                    pool.wait_ge(h_ready[2].sem, h_ready[2].at(it - 2, 1))
                    hold(pool, y_stored, y_stored.at(it - 2, 0))
                    pool.tensor_copy(x_out[:], x_res[:]).then_inc(x_kept.sem, 1)
                if m:
                    reciprocal_deviation(it - 1, 1)
                if f and m:
                    pool.wait_ge(rows.taken.sem, rows.is_taken(it, "o2"))
                    add_bias(it)
                for j in range(MID):
                    if d:
                        part_mid(it - 2, j)
                    if f and j in (2, 3):
                        part_context_columns(it, j - 2)
                    if n and j == (4 if d else 1):
                        reciprocal_deviation(it + 1, 0)
                    if m and j == 5:
                        reciprocal_deviation(it - 1, 2)

            reciprocal_deviation(0, 0)
            iterations(pool, iteration, 0)

        @block.scalar
        def _(act):
            act.sem_inc(mix_taken.sem, 2)
            act.sem_inc(y_stored.sem, 16)

            def part_weights(some):
                for n in some:
                    name, _, dst, _, _ = loads[n]
                    act.wait_ge(w_loaded[n], 16)
                    act.activation(dst[:, 0], staged[name], ACT.Copy, scale=X_W).then_inc(w_hi, 1)

            def part_product():
                for k in range(K2):
                    act.wait_ge(qk_product, k + 1)
                    act.activation(w_qk[:, 0, k], wide[:, k, 0:E], ACT.Copy,
                                   scale=X_QK / (X_W * X_W * 16)).then_inc(qk_hi, 1)

            def part_turned(it, b, dst, hi, use, scale=1.0, reverse=False):
                for k in range(K2):
                    act.wait_ge(turned.ready.sem, turned.is_ready(it, f"{use}.{k}"))
                    src = turned.bank(f"{use}.{k}")[:]
                    act.activation(dst[:, 0, k], backwards(src) if reverse else src, ACT.Copy,
                                   scale=scale).then_inc(hi.sem, 1)

            def take_mix(b, g):
                act.wait_ge(mix_ready.sem, mix_ready.at(b, g + 1))
                act.activation(mix[:, :, P * g:P * g + P].rearrange("p c (h d) -> p h c d", d=D),
                               wide[:, g].rearrange("p (h c d) -> p h c d", c=C, d=D),
                               ACT.Copy, scale=X_MIX / (X_Z * X_V)).then_inc(mix_taken.sem, 1)

            def part_values(it, b, c):
                act.wait_ge(rows.ready.sem, rows.is_ready(it, f"v{c}"))
                act.activation(val[:, 0, c:c + 2].rearrange("p c e -> p (c e)"), rows.bank(f"v{c}")[:], ACT.Copy,
                               scale=X_V / (X_H * X_W)).then_inc(val_hi.sem, 1)

            def part_context(it, b, c):
                act.wait_ge(rows.ready.sem, rows.is_ready(it, f"x{c}"))
                act.activation(vx[:, 0, c:c + 2].rearrange("p c e -> p (c e)"), rows.bank(f"x{c}")[:], ACT.Copy,
                               scale=X_VX / X_W).then_inc(vx_hi.sem, 1)

            def part_context_columns(b):
                act.wait_ge(c_loaded.sem, c_loaded.at(b, 16))
                act.wait_ge(q_ready.sem, q_ready.at(b, 0))
                for k in range(K2):
                    act.activation(cT[:, 0, k], cT_in[:, k], ACT.Copy).then_inc(c_hi.sem, 1)

            def exp_scores(it, b, c):
                act.wait_ge(score_maxed.sem, score_maxed.at(b, c + 1))
                n = P * (c + 1)
                act.activation(prob[:, c % 2, 0:n], score.bank(f"s{c}")[:, 0:n], ACT.Exp, bias=s_bias[:, c:c + 1],
                               scale=1 / (X_Q * X_H), accum_out=s_sum[:, c:c + 1]).then_inc(prob_ready.sem, 1)

            def part_prob(it, b, c):
                act.wait_ge(turned.ready.sem, turned.is_ready(it, f"pt{c}"))
                n = P * (c + 1)
                act.activation(probT[:, 0, c % 2, 0:n], turned.bank(f"pt{c}")[:, 0:n], ACT.Copy,
                               scale=X_P).then_inc(probT_hi.sem, 1)

            def tanh(it, b, j):
                act.wait_ge(mid_split.sem, mid_split.at(b, j + 1 - SLOTS))
                act.wait_ge(score.ready.sem, score.is_ready(it, f"g{j}"))
                act.activation(gated[:, j % SLOTS], score.bank(f"g{j}")[:], ACT.Tanh,
                               scale=0.5 / (X_H * X_W)).then_inc(tanh_done.sem, 1)

            def part_mid(b, j):
                act.wait_ge(gated_done.sem, gated_done.at(b, j + 1))
                act.activation(mid[:, 0, j % SLOTS], gated[:, j % SLOTS], ACT.Copy).then_inc(mid_hi.sem, 1)

            def iteration(it, f, m, d, n):
                if f:
                    act.wait_ge(z_maxed.sem, z_maxed.at(it, 2))
                    act.activation(z_exp[:], backwards(score.bank("z")[0:H, :]), ACT.Exp, bias=z_bias[:],
                                   scale=D ** -0.5 / (X_H * X_W), accum_out=z_sum[:]).then_inc(z_exped.sem, 1)
                if m:
                    take_mix(it - 1, 0)
                if d:
                    act.wait_ge(shifted.sem, shifted.at(it - 2, 2))
                    act.activation(e2[:], e2_in[:], ACT.Exp).then_inc(l_exped.sem, 1)
                    act.activation(l_exp[:], l_shift[:], ACT.Exp).then_inc(l_exped.sem, 1)
                if m:
                    take_mix(it - 1, 1)
                if f:
                    part_values(it, it, 0)
                if m:
                    part_turned(it, it - 1, mixT, mixT_hi, "mix")
                if f:
                    part_values(it, it, 2)
                if m:
                    part_context(it, it - 1, 0)
                    part_context(it, it - 1, 2)
                    for k in range(K2):
                        act.wait_ge(q_ready.sem, q_ready.at(it - 1, k + 1))
                        act.activation(qT[:, 0, k], wide[:, k], ACT.Copy, scale=X_Q / X_QK).then_inc(q_hi.sem, 1)
                if d:
                    tanh(it, it - 2, 0)
                if m:
                    part_turned(it, it - 1, h2T, h2T_hi, "h2")
                if d:
                    tanh(it, it - 2, 1)
                    part_mid(it - 2, 0)
                if m:
                    exp_scores(it, it - 1, 0)
                    exp_scores(it, it - 1, 1)
                for j in range(2, MID):
                    if d:
                        tanh(it, it - 2, j)
                        part_mid(it - 2, j - 1)
                    if m and j < C + 2:
                        part_prob(it, it - 1, j - 2)
                        if j < C:
                            exp_scores(it, it - 1, j)
                    if f and j == 3:
                        part_context_columns(it)
                if m:
                    part_turned(it, it - 1, h3T, h3T_hi, "h3")
                if d:
                    part_mid(it - 2, MID - 1)
                if n:
                    part_turned(it, it + 1, h1T, h1T_hi, "h1", reverse=True)

            part_weights(range(EARLY))
            part_turned(-1, 0, h1T, h1T_hi, "h1", reverse=True)
            part_product()
            part_weights(range(EARLY, MIDDLE))
            iteration(0, True, False, False, True)
            part_weights(range(MIDDLE, len(loads)))
            iterations(act, iteration)

        @block.vector
        def _(dve):
            turned.begin(dve, turned.taken, "h1.0")
            for banks in (score, rows):
                dve.sem_inc(banks.taken.sem, len(banks.order))
            for n in range(3):
                dve.sem_inc(h_ready[n].sem, 1)
            dve.sem_inc(q_split.sem, 2)
            dve.sem_inc(y_taken.sem, 2)

            def part_weights(some):
                for n in some:
                    name, _, dst, _, _ = loads[n]
                    dve.wait_ge(w_hi, n + 1)
                    dve.scalar_tensor_tensor(dst[:, 1], staged[name], X_W, dst[:, 0], ALU.mult,
                                             ALU.subtract).then_inc(w_lo, 1)

            def part_product():
                for k in range(K2):
                    dve.wait_ge(qk_hi, k + 1)
                    dve.scalar_tensor_tensor(w_qk[:, 1, k], wide[:, k, 0:E], X_QK / (X_W * X_W * 16), w_qk[:, 0, k],
                                             ALU.mult, ALU.subtract).then_inc(qk_lo, 1)

            def statistics(n, src, blocks):
                for c in blocks:
                    last = dve.bn_stats(stats[n][:, c], src[:, c])
                return last

            def aggregate(b, n, last):
                last.then_inc(stats_done[n].sem, 1)
                hold(dve, stats_done[n], stats_done[n].at(b, 1))
                for c in range(C):
                    last = dve.bn_aggr(mean_var[n][:, c], stats[n][:, c])
                last.then_inc(aggr_done[n].sem, 1)

            def normalise(b, it, n, src, dst, first=False):
                if not first:
                    dve.wait_ge(turned.ready.sem, turned.was_ready(it, f"h{n + 1}.1"))
                dve.wait_ge(rstd_done[n].sem, rstd_done[n].at(b, 1))
                for c in range(C):
                    last = dve.tensor_scalar(dst[:, c], src[:, c], mean_var[n][:, c, 0:1], rstd[n][:, c:c + 1],
                                             ALU.subtract, ALU.mult)
                last.then_inc(h_ready[n].sem, 1)

            def part_turned(it, b, dst, hi, use, reverse=False):
                for k in range(K2):
                    turned.take(dve, it, f"{use}.{k}")
                    dve.wait_ge(hi.sem, hi.at(b, k + 1))
                    src = turned.bank(f"{use}.{k}")[:]
                    dve.tensor_tensor(dst[:, 1, k], backwards(src) if reverse else src, dst[:, 0, k],
                                      ALU.subtract).then_inc(turned.taken.sem, 1)

            def part_values(it, b, c):
                rows.take(dve, it, f"v{c}")
                dve.wait_ge(val_hi.sem, val_hi.at(b, c // 2 + 1))
                dve.scalar_tensor_tensor(val[:, 1, c:c + 2].rearrange("p c e -> p (c e)"), rows.bank(f"v{c}")[:],
                                         X_V / (X_H * X_W), val[:, 0, c:c + 2].rearrange("p c e -> p (c e)"),
                                         ALU.mult, ALU.subtract).then_inc(rows.taken.sem, 1)

            def part_context(it, b, c):
                rows.take(dve, it, f"x{c}")
                dve.wait_ge(vx_hi.sem, vx_hi.at(b, c // 2 + 1))
                dve.scalar_tensor_tensor(vx[:, 1, c:c + 2].rearrange("p c e -> p (c e)"), rows.bank(f"x{c}")[:],
                                         X_VX / X_W, vx[:, 0, c:c + 2].rearrange("p c e -> p (c e)"),
                                         ALU.mult, ALU.subtract).then_inc(rows.taken.sem, 1)

            def score_max(it, b, c):
                score.take(dve, it, f"s{c}")
                dve.wait_ge(score.ready.sem, score.is_ready(it, f"s{c}"))
                dve.reduce_max(s_nmax[:, c:c + 1], score.bank(f"s{c}")[:, 0:P * (c + 1)], AX.X,
                               negate=True).then_inc(row_max.sem, 1)
                dve.wait_ge(row_max.sem, row_max.at(b, c + 1))
                dve.tensor_scalar(s_bias[:, c:c + 1], s_nmax[:, c:c + 1], 1 / (X_Q * X_H), None,
                                  ALU.mult).then_inc(score_maxed.sem, 1)

            def score_sum(it, b, c):
                dve.wait_ge(prob_ready.sem, prob_ready.at(b, c + 1))
                dve.tensor_scalar(s_scaled[:, c:c + 1], s_sum[:, c:c + 1], X_P * X_VX, None,
                                  ALU.mult).then_inc(prob_scaled.sem, 1)
                dve.wait_ge(prob_scaled.sem, prob_scaled.at(b, c + 1))
                dve.reciprocal(s_rsum[:, c:c + 1], s_scaled[:, c:c + 1]).then_inc(score.taken.sem, 1)

            def part_prob(it, b, c):
                turned.take(dve, it, f"pt{c}")
                dve.wait_ge(probT_hi.sem, probT_hi.at(b, c + 1))
                n = P * (c + 1)
                dve.scalar_tensor_tensor(probT[:, 1, c % 2, 0:n], turned.bank(f"pt{c}")[:, 0:n], X_P,
                                         probT[:, 0, c % 2, 0:n], ALU.mult, ALU.subtract).then_inc(turned.taken.sem, 1)

            def attended(it, c):
                rows.take(dve, it, f"p{c}")
                dve.wait_ge(score.taken.sem, score.is_taken(it, f"s{c}"))
                dve.wait_ge(rows.ready.sem, rows.is_ready(it, f"p{c}"))
                dve.scalar_tensor_tensor(x_res[:, c], rows.bank(f"p{c}")[:, 0:E], s_rsum[:, c:c + 1], x_res[:, c],
                                         ALU.mult, ALU.add).then_inc(rows.taken.sem, 1)

            def gate(it, b, j):
                to = gated[:, j % SLOTS]
                score.take(dve, it, f"g{j}")
                rows.take(dve, it, f"u{j}")
                dve.wait_ge(tanh_done.sem, tanh_done.at(b, j + 1))
                dve.scalar_tensor_tensor(to, to, 1.0, score.bank(f"g{j}")[:], ALU.add,
                                         ALU.mult).then_inc(score.taken.sem, 1)
                dve.wait_ge(score.taken.sem, score.is_taken(it, f"g{j}"))
                if j >= NSH:
                    loaded = comb_loaded[2 * (j - NSH) // PAIRS]
                    dve.wait_ge(loaded.sem, loaded.at(b, 32))
                    dve.tensor_tensor(to, to, comb_rows[:, j - NSH], ALU.mult).then_inc(opened.sem, 1)
                    dve.wait_ge(opened.sem, opened.at(b, j - NSH + 1))
                dve.wait_ge(rows.ready.sem, rows.is_ready(it, f"u{j}"))
                dve.scalar_tensor_tensor(to, to, X_MID / (2 * (X_H * X_W) ** 2), rows.bank(f"u{j}")[:], ALU.mult,
                                         ALU.mult).then_inc(rows.taken.sem, 1)
                dve.wait_ge(rows.taken.sem, rows.is_taken(it, f"u{j}"))
                dve.sem_inc(gated_done.sem, 1)

            def route(it, b):
                rows.take(dve, it, "logit")
                dve.wait_ge(rows.ready.sem, rows.is_ready(it, "logit"))
                dve.tensor_scalar(logit[:], rows.bank("logit")[:, 0:C * NE].rearrange("p (c e) -> p c e", c=C),
                                  1 / (X_H * X_W), None, ALU.mult).then_inc(rows.taken.sem, 1)
                hold(dve, rows.taken, rows.is_taken(it, "logit"))
                for c in range(C):
                    last = dve.max(top[:, c], logit[:, c])
                last.then_inc(topped.sem, 1)
                hold(dve, topped, topped.at(b, 1))
                for c in range(C):
                    last = dve.max_index(top_i[:, c], top[:, c], logit[:, c])
                last.then_inc(top_found.sem, 1)
                dve.tensor_tensor(e2_in[:], top[:, :, 1], top[:, :, 0], ALU.subtract).then_inc(shifted.sem, 1)
                dve.tensor_tensor(l_shift[:], logit[:], top[:, :, 0:1].to_broadcast([P, C, NE]),
                                  ALU.subtract).then_inc(shifted.sem, 1)
                dve.wait_ge(top_found.sem, top_found.at(b, 1))
                dve.tensor_copy(top_f[:], top_i[:, :, 0:2]).then_inc(weighed.sem, 1)

            def weigh(b):
                dve.wait_ge(l_exped.sem, l_exped.at(b, 2))
                dve.reduce_sum(l_sum[:], l_exp[:], AX.X).then_inc(weighed.sem, 1)
                dve.tensor_scalar(w_one[:], e2[:], 1.0, None, ALU.add).then_inc(weighed.sem, 1)
                dve.wait_ge(weighed.sem, weighed.at(b, 3))
                dve.scalar_tensor_tensor(w_den[:], l_sum[:], 1e-9, w_one[:], ALU.mult, ALU.add).then_inc(weighed.sem, 1)
                dve.wait_ge(weighed.sem, weighed.at(b, 4))
                dve.reciprocal(w_1[:], w_den[:]).then_inc(weighed.sem, 1)
                dve.wait_ge(weighed.sem, weighed.at(b, 5))
                dve.tensor_tensor(w_2[:], w_1[:], e2[:], ALU.mult).then_inc(weighed.sem, 1)
                dve.wait_ge(weighed.sem, weighed.at(b, 6))
                for c in range(C):
                    dve.tensor_scalar(comb1[:, c], expert_no[:], top_f[:, c, 0:1], w_1[:, c:c + 1],
                                      ALU.is_equal, ALU.mult)
                    last = dve.tensor_scalar(comb2[:, c], expert_no[:], top_f[:, c, 1:2], w_2[:, c:c + 1],
                                             ALU.is_equal, ALU.mult)
                last.then_inc(weighed.sem, 1)
                dve.wait_ge(weighed.sem, weighed.at(b, 7))
                dve.tensor_tensor(comb[:], comb1[:], comb2[:], ALU.add).then_inc(weighed.sem, 1)

            def take_comb(it):
                turned.take(dve, it, "combT")
                dve.wait_ge(turned.ready.sem, turned.is_ready(it, "combT"))
                dve.tensor_copy(combT[:], turned.bank("combT")[0:NE, :]).then_inc(turned.taken.sem, 1)

            def x_statistics(b):
                dve.wait_ge(x_loaded.sem, x_loaded.at(b, 16))
                aggregate(b, 0, statistics(0, x_in, range(C)))

            def iteration(it, f, m, d, n):
                if f:
                    score.take(dve, it, "z")
                    dve.wait_ge(score.ready.sem, score.is_ready(it, "z"))
                    dve.reduce_max(z_nmax[:], score.bank("z")[0:H, :], AX.X, negate=True).then_inc(z_maxed.sem, 1)
                    dve.wait_ge(z_maxed.sem, z_maxed.at(it, 1))
                    dve.tensor_scalar(z_bias[:], z_nmax[:], D ** -0.5 / (X_H * X_W), None,
                                      ALU.mult).then_inc(z_maxed.sem, 1)
                if d:
                    route(it, it - 2)
                    if not m:
                        score.take(dve, it, "g0")
                        rows.take(dve, it, "u0")
                if f:
                    dve.wait_ge(z_exped.sem, z_exped.at(it, 1))
                    dve.reciprocal(z_rsum[:], z_sum[:]).then_inc(score.taken.sem, 1)
                if d:
                    weigh(it - 2)
                if f:
                    part_values(it, it, 0)
                if m:
                    part_turned(it, it - 1, mixT, mixT_hi, "mix")
                if f:
                    part_values(it, it, 2)
                if m:
                    part_context(it, it - 1, 0)
                    dve.wait_ge(x_biased.sem, x_biased.at(it - 1, 1))
                    dve.wait_ge(x_kept.sem, x_kept.at(it - 2, 1))
                    for c in range(0, C, 2):
                        rows.take(dve, it, f"o{c}")
                        dve.wait_ge(rows.ready.sem, rows.is_ready(it, f"o{c}"))
                        dve.scalar_tensor_tensor(x_res[:, c:c + 2],
                                                 rows.bank(f"o{c}")[:].rearrange("p (c e) -> p c e", c=2),
                                                 1 / (X_MIX * X_W), x_bo[:, c:c + 2], ALU.mult,
                                                 ALU.add).then_inc(rows.taken.sem, 1)
                        hold(dve, rows.taken, rows.is_taken(it, f"o{c}"))
                        last = statistics(1, x_res, range(c, c + 2))
                    aggregate(it - 1, 1, last)
                    part_context(it, it - 1, 2)
                    if d:
                        take_comb(it)
                    for k in range(K2):
                        dve.wait_ge(q_hi.sem, q_hi.at(it - 1, k + 1))
                        dve.scalar_tensor_tensor(qT[:, 1, k], wide[:, k], X_Q / X_QK, qT[:, 0, k], ALU.mult,
                                                 ALU.subtract).then_inc(q_split.sem, 1)
                    normalise(it - 1, it, 1, x_res, h2)
                if d:
                    gate(it, it - 2, 0)
                    if not m:
                        take_comb(it)
                if m:
                    part_turned(it, it - 1, h2T, h2T_hi, "h2")
                if d:
                    gate(it, it - 2, 1)
                if m:
                    for c in range(2):
                        score_max(it, it - 1, c)
                        score_sum(it, it - 1, c)
                for j in range(2, MID):
                    if d:
                        gate(it, it - 2, j)
                    if m:
                        if not d and j - 2 < C:
                            part_prob(it, it - 1, j - 2)
                        if 0 <= j - 3 < C:
                            attended(it, j - 3)
                        if 0 <= j - 4 < C - 1:
                            hold(dve, rows.taken, rows.is_taken(it, f"p{j - 4}"))
                            statistics(2, x_res, [j - 4])
                        if d and j - 2 < C:
                            part_prob(it, it - 1, j - 2)
                        if j < C:
                            score_max(it, it - 1, j)
                            score_sum(it, it - 1, j)
                        if j == 6:
                            hold(dve, rows.taken, rows.is_taken(it, "p3"))
                            aggregate(it - 1, 2, statistics(2, x_res, [C - 1]))
                        if j == 7:
                            normalise(it - 1, it, 2, x_res, h3)
                    if n:
                        if j == 5:
                            x_statistics(it + 1)
                        if j == 8:
                            normalise(it + 1, it, 0, x_in, h1)
                if m:
                    part_turned(it, it - 1, h3T, h3T_hi, "h3")
                if n:
                    part_turned(it, it + 1, h1T, h1T_hi, "h1", reverse=True)
                if d:
                    dve.wait_ge(x_kept.sem, x_kept.at(it - 2, 1))
                    dve.wait_ge(y_ready.sem, y_ready.at(it - 2, 1))
                    for g in range(2):
                        last = dve.scalar_tensor_tensor(
                            x_out[:, 2 * g:2 * g + 2], wide[:, g].rearrange("p (c e) -> p c e", c=2),
                            1 / (X_MID * X_W), x_out[:, 2 * g:2 * g + 2], ALU.mult, ALU.add)
                    last.then_inc(y_taken.sem, 1)
                for banks in (turned, score, rows):
                    banks.reach(dve, banks.taken, it)

            x_statistics(0)
            part_weights(range(2))
            normalise(0, -1, 0, x_in, h1, first=True)
            part_weights(range(2, EARLY))
            part_turned(-1, 0, h1T, h1T_hi, "h1", reverse=True)
            turned.reach(dve, turned.taken, -1)
            part_product()
            part_weights(range(EARLY, MIDDLE))
            iteration(0, True, False, False, True)
            part_weights(range(MIDDLE, len(loads)))
            iterations(dve, iteration)

        @block.tensor
        def _(pe):
            turned.begin(pe, turned.ready, "h1.0")
            for banks in (score, rows):
                pe.sem_inc(banks.ready.sem, len(banks.order))
            pe.sem_inc(q_ready.sem, 2)
            pe.wait_ge(const_made, 9)

            def turn(it, use, src):
                for k in range(K2):
                    turned.fill(pe, it, f"{use}.{k}")
                    for c in range(C):
                        last = pe.transpose(turned.bank(f"{use}.{k}")[:, P * c:P * c + P], src[:, c, P * k:P * k + P],
                                            ident[:])
                    last.then_inc(turned.ready.sem, 1)

            def project(it, use, src, w):
                rows.fill(pe, it, use)
                for c in range(2):
                    at = P * (int(use[-1]) + c)
                    for k in range(K2):
                        last = three_passes(pe, rows.bank(use)[:, E * c:E * c + E], parts(src, k, slice(at, at + P)),
                                            parts(w, k, slice(None)), start=(k == 0), stop=(k == K2 - 1))
                last.then_inc(rows.ready.sem, 1)

            def toeplitz(it, b, g):
                if g == 0:
                    pe.wait_ge(toep_loaded.sem, toep_loaded.at(b, 32))
                    pe.wait_ge(rows.taken.sem, rows.is_taken(it - 1, "v2"))
                    pe.wait_ge(y_taken.sem, y_taken.at(b, -1))
                for n in range(H // 2):
                    head = H // 2 * g + n
                    acc = wide[:, g, C * D * n:C * D * (n + 1)].rearrange("p (c d) -> p c d", c=C)
                    for delta in range(C):
                        last = three_passes(pe, acc[:, delta:C, :], parts(toep, head, slice(P * delta, P * delta + P)),
                                            parts(val, slice(0, C - delta), slice(D * head, D * head + D)),
                                            start=(delta == 0), stop=(delta == C - 1), skip_group_check=True)
                last.then_inc(mix_ready.sem, 1)

            def scores(it, c):
                n = P * (c + 1)
                to = score.bank(f"s{c}")
                score.fill(pe, it, f"s{c}")
                for k in range(K2):
                    three_passes(pe, to[:, 0:n], parts(qT, k, slice(P * c, P * c + P)), parts(h2T, k, slice(0, n)),
                                 start=(k == 0), stop=False, skip_group_check=True)
                pe.matmul(to[:, n - P:n], ident16[:], future[:], start=False, stop=True,
                          skip_group_check=True).then_inc(score.ready.sem, 1)

            def turn_probs(it, b, c):
                turned.fill(pe, it, f"pt{c}")
                pe.wait_ge(prob_ready.sem, prob_ready.at(b, c + 1))
                for t in range(c + 1):
                    last = pe.transpose(turned.bank(f"pt{c}")[:, P * t:P * t + P], prob[:, c % 2, P * t:P * t + P],
                                        ident[:])
                last.then_inc(turned.ready.sem, 1)

            def attend(it, c):
                rows.fill(pe, it, f"p{c}")
                pe.wait_ge(turned.taken.sem, turned.is_taken(it, f"pt{c}"))
                for t in range(c + 1):
                    last = three_passes(pe, rows.bank(f"p{c}")[:, 0:E], parts(probT, c % 2, slice(P * t, P * t + P)),
                                        parts(vx, t, slice(None)), start=(t == 0), stop=(t == c))
                last.then_inc(rows.ready.sem, 1)

            def gate_up(it, j):
                for at, banks, use in ((0, score, f"g{j}"), (P, rows, f"u{j}")):
                    banks.fill(pe, it, use)
                    for k in range(K2):
                        last = three_passes(pe, banks.bank(use)[:],
                                            parts(w_gu, k, slice(2 * P * j + at, 2 * P * j + at + P)),
                                            parts(h3T, k, slice(None)), start=(k == 0), stop=(k == K2 - 1))
                    last.then_inc(banks.ready.sem, 1)

            def turn_comb(it):
                turned.fill(pe, it, "combT")
                pe.wait_ge(weighed.sem, weighed.at(it - 2, 8))
                for c in range(C):
                    last = pe.transpose(turned.bank("combT")[0:NE, P * c:P * c + P], comb[:, c], ident[:])
                last.then_inc(turned.ready.sem, 1)

            def down(b, j):
                pe.wait_ge(mid_split.sem, mid_split.at(b, j + 1))
                for c in range(C):
                    last = three_passes(pe, wide[:, c // 2, E * (c % 2):E * (c % 2) + E],
                                        parts(mid, j % SLOTS, slice(P * c, P * c + P)), parts(w_d, j, slice(None)),
                                        start=(j == 0 and c % 2 == 0), stop=(j == MID - 1), skip_group_check=True)
                if j == MID - 1:
                    last.then_inc(y_ready.sem, 1)

            def iteration(it, f, m, d, n):
                if d:
                    rows.fill(pe, it, "logit")
                    pe.wait_ge(turned.taken.sem, turned.is_taken(it - 1, "h3.1"))
                    for c in range(C):
                        for k in range(K2):
                            last = three_passes(pe, rows.bank("logit")[:, NE * c:NE * c + NE],
                                                parts(h3T, k, slice(P * c, P * c + P)), parts(w_r, k, slice(None)),
                                                start=(k == 0), stop=(k == K2 - 1))
                    last.then_inc(rows.ready.sem, 1)
                if f:
                    score.fill(pe, it, "z")
                    pe.wait_ge(turned.taken.sem, turned.is_taken(it - 1, "h1.1"))
                    for k in range(K2):
                        last = three_passes(pe, score.bank("z")[0:H, :], parts(w_a, k, slice(None)),
                                            parts(h1T, k, slice(None)), start=(k == 0), stop=(k == K2 - 1))
                    last.then_inc(score.ready.sem, 1)
                if m:
                    toeplitz(it, it - 1, 0)
                    toeplitz(it, it - 1, 1)
                if f:
                    project(it, "v0", h1T, w_v)
                if m:
                    pe.wait_ge(mix_taken.sem, mix_taken.at(it - 1, 2))
                    turn(it, "mix", mix)
                if f:
                    project(it, "v2", h1T, w_v)
                if m:
                    pe.wait_ge(c_split.sem, c_split.at(it - 1, K2))
                    project(it, "x0", cT, w_vx)
                    pe.wait_ge(turned.taken.sem, turned.is_taken(it, "mix.1"))
                    project(it, "o0", mixT, w_o)
                    project(it, "o2", mixT, w_o)
                    project(it, "x2", cT, w_vx)
                    if d:
                        turn_comb(it)
                    for h in range(K2):
                        for k in range(K2):
                            last = three_passes(pe, wide[:, h], parts(w_qk, k, slice(P * h, P * h + P)),
                                                parts(cT, k, slice(None)), start=(k == 0), stop=(k == K2 - 1))
                        last.then_inc(q_ready.sem, 1)
                if d:
                    gate_up(it, 0)
                    if not m:
                        turn_comb(it)
                if m:
                    pe.wait_ge(h_ready[1].sem, h_ready[1].at(it - 1, 1))
                    turn(it, "h2", h2)
                if d:
                    gate_up(it, 1)
                if m:
                    pe.wait_ge(q_split.sem, q_split.at(it - 1, 2))
                    pe.wait_ge(turned.taken.sem, turned.is_taken(it, "h2.1"))
                    scores(it, 0)
                    scores(it, 1)
                if d and m:
                    down(it - 2, 0)
                for j in range(2, MID):
                    if d:
                        gate_up(it, j)
                    if m:
                        if d and 0 <= j - 3 < C:
                            attend(it, j - 3)
                        if j - 2 < C:
                            turn_probs(it, it - 1, j - 2)
                        if j < C:
                            scores(it, j)
                        if not d and 0 <= j - 3 < C:
                            attend(it, j - 3)
                    if d and m and j < C:
                        down(it - 2, j - 1)
                    if d and not m and j == 2:
                        pe.wait_ge(y_taken.sem, y_taken.at(it - 2, 0))
                    if d and (not m or j > C):
                        down(it - 2, j - 2)
                if m:
                    pe.wait_ge(h_ready[2].sem, h_ready[2].at(it - 1, 1))
                    turn(it, "h3", h3)
                if d:
                    down(it - 2, MID - 2)
                if n:
                    pe.wait_ge(h_ready[0].sem, h_ready[0].at(it + 1, 1))
                    turn(it, "h1", h1)
                if d:
                    down(it - 2, MID - 1)
                for banks in (turned, score, rows):
                    banks.reach(pe, banks.ready, it)

            pe.wait_ge(h_ready[0].sem, h_ready[0].at(0, 1))
            turn(-1, "h1", h1)
            turned.reach(pe, turned.ready, -1)
            pe.wait_ge(w_lo, EARLY)
            for n in range(K2):
                for k in range(K2):
                    last = three_passes(pe, wide[:, n, 0:E], parts(w_q, k, slice(P * n, P * n + P)),
                                        parts(w_k, k, slice(None)), start=(k == 0), stop=(k == K2 - 1))
                last.then_inc(qk_product, 1)
            iteration(0, True, False, False, True)
            pe.wait_ge(qk_lo, 2)
            pe.wait_ge(w_lo, MIDDLE)
            iteration(1, True, True, False, True)
            pe.wait_ge(w_lo, len(loads))
            with pe.Fori(2, B - 1) as it:
                iteration(it, True, True, True, True)
            iteration(B - 1, True, True, True, False)
            iteration(B, False, True, True, False)
            iteration(B + 1, False, False, True, False)


def kernel(x, ctx_1024, L0_attn_W_A, L0_attn_W_V, L0_attn_W_O, L0_attn_b_O, L0_xattn_WK, L0_xattn_WV,
           L0_xattn_WQ, L0_ffn_router_w, L0_ffn_wg_r, L0_ffn_wu_r, L0_ffn_wd_r, L0_ffn_wg_s, L0_ffn_wu_s,
           L0_ffn_wd_s):
    import numpy as np
    import concourse.bacc as bacc
    from concourse.bass_utils import run_bass_kernel_spmd

    def gate_up_columns(g, u):
        n, d, m = g.shape
        g, u = (np.transpose(np.asarray(w), (1, 0, 2)).reshape(d, n * m // P, 1, P) for w in (g, u))
        return np.ascontiguousarray(np.concatenate([g, u], axis=2).reshape(d, 2 * n * m))

    arrays = {
        "x": np.asarray(x),
        "ctxT": np.ascontiguousarray(np.transpose(np.asarray(ctx_1024), (0, 2, 1))),
        "wa": np.ascontiguousarray(np.asarray(L0_attn_W_A).T),
        "wv": np.ascontiguousarray(np.asarray(L0_attn_W_V).T),
        "wo": np.ascontiguousarray(np.asarray(L0_attn_W_O).T),
        "bo": np.asarray(L0_attn_b_O),
        "wq": np.ascontiguousarray(np.asarray(L0_xattn_WQ).T),
        "wk": np.ascontiguousarray(np.asarray(L0_xattn_WK).T),
        "wvx": np.asarray(L0_xattn_WV),
        "rw": np.asarray(L0_ffn_router_w),
        "gu_s": gate_up_columns(L0_ffn_wg_s, L0_ffn_wu_s),
        "wd_s": np.asarray(L0_ffn_wd_s).reshape(-1, E),
        "gu_r": gate_up_columns(L0_ffn_wg_r, L0_ffn_wu_r),
        "wd_r": np.asarray(L0_ffn_wd_r).reshape(-1, E),
    }
    nc = bacc.Bacc("TRN2", target_bir_lowering=False, num_devices=1)
    args = [nc.dram_tensor(f"in_{n}", a.shape, mybir.dt.from_np(a.dtype), kind="ExternalInput").ap()
            for n, a in arrays.items()]
    out = nc.dram_tensor("out_0", (B, S, E), F32, kind="ExternalOutput").ap()
    decoder_layer(nc, *args, out)
    r = run_bass_kernel_spmd(nc, [{f"in_{n}": a for n, a in arrays.items()}], core_ids=[0])
    return r.results[0]["out_0"]
```
